# Optimizing a Trainium2 kernel written in Bass

```python
import numpy as np
import jax
import jax.numpy as jnp

def _softmax(x, axis=-1):
    return jax.nn.softmax(x, axis=axis)

def _gelu(x):
    return jax.nn.gelu(x, approximate=True)

def _silu(x):
    return jax.nn.silu(x)

def _sigmoid(x):
    return jax.nn.sigmoid(x)

def _layernorm(x, axis=-1, eps=1e-05):
    m = jnp.mean(x, axis=axis, keepdims=True)
    v = jnp.var(x, axis=axis, keepdims=True)
    return (x - m) / jnp.sqrt(v + eps)

def _scatter_add(tgt, idx, src, axis=0):
    return tgt.at[idx].add(src)

def _segment_sum(src, seg, n):
    return jax.ops.segment_sum(src, seg, n)
kernel_name = 'mk_macaron_d1_jaxref_r4_764642'

def setup_inputs(seed: int=0):
    np.random.seed(seed)
    _w = jnp.asarray

    def _L0_attn_setup():
        import jax, jax.numpy as jnp
        import numpy as np
        B, S, D, H = (2, 512, 256, 16)
        MASK_VAL = -50000.0
        key = jax.random.key(seed)
        k1, k2, k3, k4 = jax.random.split(key, 4)
        s = 1.0 / np.sqrt(D)
        return {'x': jax.random.normal(k1, (B, S, D), dtype=jnp.float32), 'Wq': jax.random.normal(k2, (D, D), dtype=jnp.float32) * s, 'Wkv': jax.random.normal(k3, (D, 2 * D), dtype=jnp.float32) * s, 'Wo': jax.random.normal(k4, (D, D), dtype=jnp.float32) * s}
    _L0_attn_in = _L0_attn_setup()

    def _L0_ffn_setup():
        import jax, jax.numpy as jnp
        import numpy as np
        LN_EPS = 1e-05

        def _layernorm(x, g, b):
            m = jnp.mean(x, axis=-1, keepdims=True)
            v = jnp.mean(jnp.square(x - m), axis=-1, keepdims=True)
            return (x - m) * jax.lax.rsqrt(v + LN_EPS) * g + b
        K_TOP = 2
        key = jax.random.key(seed)
        ks = jax.random.split(key, 4)
        B, N, D, E = (8, 512, 256, 4)
        s = 0.02
        return {'x': jax.random.normal(ks[0], (B, N, D), dtype=jnp.float32), 'gate_W': jax.random.normal(ks[1], (D, E), dtype=jnp.float32) * s, 'gate_b': jnp.zeros((E,), jnp.float32), 'W1': jax.random.normal(ks[2], (E, D, D), dtype=jnp.float32) * s, 'b1': jnp.zeros((E, D), jnp.float32), 'g1': jnp.ones((E, D), jnp.float32), 'be1': jnp.zeros((E, D), jnp.float32), 'W2': jax.random.normal(ks[3], (E, D, D), dtype=jnp.float32) * s, 'b2': jnp.zeros((E, D), jnp.float32), 'g2': jnp.ones((E, D), jnp.float32), 'be2': jnp.zeros((E, D), jnp.float32)}
    _L0_ffn_in = _L0_ffn_setup()
    _d = {'L0_attn_x': _L0_attn_in['x'], 'L0_attn_Wq': _L0_attn_in['Wq'], 'L0_attn_Wkv': _L0_attn_in['Wkv'], 'L0_attn_Wo': _L0_attn_in['Wo'], 'L0_ffn_gate_W': _L0_ffn_in['gate_W'], 'L0_ffn_gate_b': _L0_ffn_in['gate_b'], 'L0_ffn_W1': _L0_ffn_in['W1'], 'L0_ffn_b1': _L0_ffn_in['b1'], 'L0_ffn_g1': _L0_ffn_in['g1'], 'L0_ffn_be1': _L0_ffn_in['be1'], 'L0_ffn_W2': _L0_ffn_in['W2'], 'L0_ffn_b2': _L0_ffn_in['b2'], 'L0_ffn_g2': _L0_ffn_in['g2'], 'L0_ffn_be2': _L0_ffn_in['be2']}
    _x0 = _d['L0_attn_x']
    _d['L0_attn_x'] = jax.random.normal(jax.random.fold_in(jax.random.key(seed), 1), (16, 512, 256), dtype=_x0.dtype)
    del _x0
    return _d

def reference(L0_attn_x, L0_attn_Wq, L0_attn_Wkv, L0_attn_Wo, L0_ffn_gate_W, L0_ffn_gate_b, L0_ffn_W1, L0_ffn_b1, L0_ffn_g1, L0_ffn_be1, L0_ffn_W2, L0_ffn_b2, L0_ffn_g2, L0_ffn_be2):

    def _L0_attn_ref(x, Wq, Wkv, Wo):
        import jax, jax.numpy as jnp
        import numpy as np
        B, S, D, H = (2, 512, 256, 16)
        MASK_VAL = -50000.0
        b, sl, d = x.shape
        h = H
        hd = d // h
        scale = hd ** (-0.5)
        q = x @ Wq
        kv = x @ Wkv
        k, v = jnp.split(kv, 2, axis=-1)
        q = q.reshape(b, sl, h, hd).transpose(0, 2, 1, 3)
        k = k.reshape(b, sl, h, hd).transpose(0, 2, 1, 3)
        v = v.reshape(b, sl, h, hd).transpose(0, 2, 1, 3)
        dots = jnp.einsum('bhid,bhjd->bhij', q * scale, k)
        causal = jnp.tril(jnp.ones((sl, sl), dtype=bool))
        dots = jnp.where(causal, dots, MASK_VAL)
        attn = jax.nn.softmax(dots, axis=-1)
        out = jnp.einsum('bhij,bhjd->bihd', attn, v).reshape(b, sl, d)
        return out @ Wo

    def _L0_ffn_ref(x, gate_W, gate_b, W1, b1, g1, be1, W2, b2, g2, be2):
        import jax, jax.numpy as jnp
        import numpy as np
        LN_EPS = 1e-05

        def _layernorm(x, g, b):
            m = jnp.mean(x, axis=-1, keepdims=True)
            v = jnp.mean(jnp.square(x - m), axis=-1, keepdims=True)
            return (x - m) * jax.lax.rsqrt(v + LN_EPS) * g + b
        K_TOP = 2
        B, N, D = x.shape
        BN = B * N
        xf = x.reshape(BN, D)
        gate_scores = xf @ gate_W + gate_b
        topk_scores, topk_idx = jax.lax.top_k(gate_scores, K_TOP)
        weights = jax.nn.softmax(topk_scores, axis=-1)

        def expert(w1, bb1, gg1, bbe1, w2, bb2, gg2, bbe2):
            h = jax.nn.relu(_layernorm(xf @ w1 + bb1, gg1, bbe1))
            return _layernorm(h @ w2 + bb2, gg2, bbe2)
        all_out = jax.vmap(expert)(W1, b1, g1, be1, W2, b2, g2, be2)
        exp_out = all_out[topk_idx, jnp.arange(BN)[:, None]]
        out = jnp.sum(weights[..., None] * exp_out, axis=1)
        return (out + xf).reshape(B, N, D)
    x = L0_attn_x
    x = x + 0.5 * _L0_ffn_ref(_layernorm(x, axis=-1), L0_ffn_gate_W, L0_ffn_gate_b, L0_ffn_W1, L0_ffn_b1, L0_ffn_g1, L0_ffn_be1, L0_ffn_W2, L0_ffn_b2, L0_ffn_g2, L0_ffn_be2)
    x = x + _L0_attn_ref(_layernorm(x, axis=-1), L0_attn_Wq, L0_attn_Wkv, L0_attn_Wo)
    x = x + 0.5 * _L0_ffn_ref(_layernorm(x, axis=-1), L0_ffn_gate_W, L0_ffn_gate_b, L0_ffn_W1, L0_ffn_b1, L0_ffn_g1, L0_ffn_be1, L0_ffn_W2, L0_ffn_b2, L0_ffn_g2, L0_ffn_be2)
    return x

_drawn_inputs = setup_inputs


def setup_inputs(seed=0):
    import zlib

    import numpy as np

    out = dict(_drawn_inputs(seed))
    spreads = {'L0_ffn_gate_b': (0.0, 0.1),
     'L0_ffn_b1': (0.0, 0.1),
     'L0_ffn_g1': (1.0, 0.2),
     'L0_ffn_be1': (0.0, 0.1),
     'L0_ffn_b2': (0.0, 0.1),
     'L0_ffn_g2': (1.0, 0.2),
     'L0_ffn_be2': (0.0, 0.1)}
    factors = {}
    for name, (base, spread) in spreads.items():
        noise = np.random.default_rng([zlib.crc32(name.encode()), seed]).standard_normal(out[name].shape)
        drawn = base * np.exp(spread * noise) if base else spread * noise
        out[name] = jnp.asarray(drawn.astype(out[name].dtype))
    for name, factor in factors.items():
        out[name] = (out[name] * factor).astype(out[name].dtype)
    return out
```

```python
import concourse.bass as bass
from concourse import mybir
from contextlib import ExitStack


def macaron_kernel(nc, x, Wq, Wkv, Wo, gate_W, gate_b, W1, b1, g1, be1, W2, b2, g2, be2, out):
    fp32, fp32r, bf16 = mybir.dt.float32, mybir.dt.float32r, mybir.dt.bfloat16
    ALU, ACT, AX = mybir.AluOpType, mybir.ActivationFunctionType, mybir.AxisListType

    NSEQ, S, D = x.shape
    NEXP = gate_W.shape[1]
    P = 128
    H, HD = 16, D // 16
    T = S // P
    C = D // P
    HC = H // C
    QUAD = 4
    SCALE = float(HD) ** -0.5
    LN_EPS = 1e-5
    MASKED = -1e30
    NBLK = T * (T + 1) // 2
    WIDE = NBLK * P
    QPART = (0, 0, 0, 1, 1, 2)
    KPART = (0, 1, 2, 0, 1, 0)
    G = len(QPART)
    KR = G * HD
    MCOL = {3: 0, 2: 4 * P, 0: 7 * P, 1: 8 * P}
    ECOL = {0: 0, 1: 4 * P, 3: 7 * P, 2: 8 * P}

    MPART = ((3,), (2, 0, 1))
    EPART = ((0,), (1, 3, 2))
    PCOL = (0, T * P, WIDE)

    ctx = ExitStack()
    with ctx:
        def sb(name, shape, dt=fp32):
            return ctx.enter_context(nc.sbuf_tensor(name, shape, dt))

        def ps(name, shape, dt=fp32):
            return ctx.enter_context(nc.psum_tensor(name, shape, dt))

        WKD = NEXP * C * D
        w1 = [sb(f"w1_{p}", [P, NEXP, C, D], fp32r) for p in "hl"]
        w2 = [sb(f"w2_{p}", [P, NEXP, C, D], fp32r) for p in "hl"]
        wqkv = [sb(f"wqkv_{p}", [P, C, 3 * D], fp32r) for p in "hl"]
        wo = [sb(f"wo_{p}", [P, C, D], fp32r) for p in "hl"]
        gw = [sb(f"gw_{p}", [P, C, NEXP], fp32r) for p in "hl"]
        gb = sb("gb", [NEXP, 1])
        bias = sb("bias", [P, NEXP, D], bf16)
        ones3 = [sb(f"ones3_{m}", [P, P], bf16) for m in range(2)]
        g1c = sb("g1c", [P, NEXP, C])
        be1c = sb("be1c", [P, NEXP, C])
        g2b = sb("g2b", [P, NEXP, D])
        be2b = sb("be2b", [P, NEXP, D])
        identf = sb("identf", [P, P])
        identb = sb("identb", [P, P], bf16)
        mask_q = sb("mask_q", [P, P], bf16)
        mask_k = sb("mask_k", [P, P], bf16)
        neghalf = sb("neghalf", [P, 2 * T])
        lower = sb("lower", [P, T, NEXP, NEXP])
        acc = {k: sb(f"z_summed_{k}", [P, T, D]) for k in "AB"}
        xn = {k: sb(f"ln_ready_{k}", [P, T, D]) for k in "AB"}
        xn["Q"], on = xn["B"], xn["A"]
        xt = {k: [sb(f"xt{k}_{p}", [P, C, S], fp32r) for p in "hl"] for k in "AB"}
        xt["Q"], xt["O"] = xt["A"], xt["B"]
        mv = {k: sb(f"mv{k}", [P, T, 2]) for k in "ABQ"}
        st6 = {k: sb(f"st6{k}", [P, T, 6]) for k in "ABQ"}
        rstd = {k: sb(f"rstd{k}", [P, T]) for k in "ABQ"}
        rtmp = {k: sb(f"rtmp{k}", [P, T]) for k in "ABQ"}
        gs = {k: sb(f"gs{k}", [P, T, NEXP]) for k in "AB"}
        gmax = {k: sb(f"gmax{k}", [P, T]) for k in "AB"}
        gcmp = sb("gcmp", [P, T, NEXP, NEXP])
        gcmq = sb("gcmq", [P, T, NEXP, NEXP])
        grank = {k: sb(f"grank{k}", [P, T, NEXP]) for k in "AB"}
        gexp = {k: sb(f"gexp{k}", [P, T, NEXP]) for k in "AB"}
        gsum = {k: sb(f"gsum{k}", [P, T]) for k in "AB"}
        wgt = {k: sb(f"wgt{k}", [P, T, NEXP]) for k in "AB"}
        ss1 = {k: sb(f"ss1{k}", [P, T]) for k in "AB"}
        ss2 = {k: sb(f"ss2{k}", [P, T]) for k in "AB"}
        rs1 = {k: sb(f"rs1{k}", [P, T]) for k in "AB"}
        rs2 = {k: sb(f"rs2{k}", [P, T]) for k in "AB"}
        tmp1 = {k: sb(f"tmp1{k}", [P, T]) for k in "AB"}
        tmp2 = {k: sb(f"tmp2{k}", [P, T]) for k in "AB"}
        wst = {k: sb(f"wst{k}", [P, T]) for k in "AB"}
        junk = sb("junk", [P, T, D], bf16)
        hh = sb("hh", [P, C, S], fp32r)
        hl = sb("hl", [P, C, S], fp32r)
        qs = [sb(f"qs{s}", [P, H, S], bf16) for s in range(2)]
        ks = [sb(f"ks{s}", [P, H, S], bf16) for s in range(2)]
        va = [sb(f"va{s}", [P, T, H, HD + 1]) for s in range(2)]
        bm = sb("bm", [P, H, NBLK])
        nm = sb("nm", [P, T, H])
        nmr = sb("nmr", [P, T, H])
        nmp = sb("nmp", [P, T, 3, H], bf16)
        nmt = sb("nmt", [3 * H, S], bf16)
        ot = sb("ot", [P, S])
        rden = sb("rden", [P, T, QUAD])
        NPT = 5
        O_HF = T * D
        O_U = O_HF + C * S
        O_QK = O_U + T * D
        N_QK = 3 * C * S // 2
        O_R = O_QK + 2 * N_QK
        space = sb("space", [P, max(O_R + S, NPT * WIDE)])
        pt = space[:, 0:NPT * WIDE].rearrange("p (a n) -> p a n", a=NPT)
        yn = space[:, 0:O_HF].rearrange("p (t n) -> p t n", t=T)
        res = yn
        hf = space[:, O_HF:O_U].rearrange("p (c n) -> p c n", c=C)
        u = space[:, O_U:O_QK].rearrange("p (t n) -> p t n", t=T)
        qkp = [space[:, O_QK + n * N_QK:O_QK + (n + 1) * N_QK].bitcast(bf16).rearrange(
            "p (a c s) -> p a c s", a=3, c=C) for n in range(2)]
        qkr = space[:, O_R:O_R + S]
        gt = {"A": qkr[0:NEXP, :], "B": space[0:NEXP, O_U:O_U + S]}

        bank = ps("bank", [P, 8, 512])
        tps = bank[:, 3:5, :]
        gps = {"A": bank[:, 5, :], "B": bank[:, 6, :]}
        mps = bank[:, 0:3, :].rearrange("p b n -> p (b n)")
        eps_ = bank[:, 3:6, :].rearrange("p b n -> p (b n)")
        ops = bank[:, 6, :]
        rps = bank[:, 7, :]
        qkb = [bank[:, n, :] for n in (0, 1, 2, 5)]

        per = {}
        sem = {}

        def mk(name, n):
            per[name] = n
            sem[name] = ctx.enter_context(nc.semaphore(name))

        for k in "AB":
            mk(f"y_ready_{k}", 2 * NEXP)
            mk(f"y_squares_{k}", NEXP)
            mk(f"y_var_{k}", NEXP)
            mk(f"y_rstd_{k}", NEXP)
            mk(f"y_normed_{k}", 2 * NEXP)
            mk(f"y_turned_{k}", 2 * NEXP)
            mk(f"h_ready_{k}", 2 * NEXP)
            mk(f"h_high_{k}", 2 * NEXP)
            mk(f"h_low_{k}", 2 * NEXP)
            mk(f"z_ready_{k}", 2 * NEXP)
            mk(f"z_squares_{k}", NEXP)
            mk(f"z_var_{k}", NEXP)
            mk(f"z_rstd_{k}", NEXP)
            mk(f"z_factor_{k}", NEXP)
            mk(f"z_scaled_{k}", 2 * NEXP)
            mk(f"z_shifted_{k}", NEXP)
            mk(f"z_summed_{k}", NEXP)
            mk(f"sum_begun_{k}", 1)
            mk(f"gate_ready_{k}", 1)
            mk(f"gate_biased_{k}", 1)
            mk(f"gate_turned_{k}", 1)
            mk(f"gate_step_{k}", 10)
            mk(f"gate_exp_{k}", 1)
        for k in "ABQ":
            mk(f"ln_stats_{k}", 1)
            mk(f"ln_parts_{k}", 1)
            mk(f"ln_var_{k}", 1)
            mk(f"ln_rstd_{k}", 1)
            mk(f"ln_ready_{k}", 1)
            mk(f"x_turned_{k}", C)
            mk(f"x_high_{k}", C)
            mk(f"x_low_{k}", C)
        mk("x_loaded", 16)
        mk("out_stored", 16)
        mk("x1_kept", 16)
        mk("x1_back", 16)
        mk("qk_ready", 2 * C)
        mk("qk_part1", 2 * C)
        mk("qk_rest", 2 * C)
        mk("qk_part2", 2 * C)
        mk("qk_part3", 2 * C)
        mk("v_ready", 2)
        mk("v_copied", 2)
        mk("stacks_placed", 16 * 2 * G * HC)
        mk("queries_scored", 2 * H)
        mk("block_maxima", 2 * H)
        mk("maxima_ready", 1)
        mk("maxima_part", 3)
        mk("maxima_rest", 2)
        mk("maxima_turned", 1)
        mk("maxima_copied", 1)
        mk("maxima_placed", 16 * 3)
        mk("keys_scored", 2 * H)
        mk("exp_ready", 2 * H)
        mk("pv_ready", QUAD)
        mk("pv_copied", QUAD)
        mk("pv_turned", QUAD)
        mk("sums_inverted", QUAD)
        mk("pv_normed", QUAD)
        mk("x_turned_O", C)
        mk("x_high_O", C)
        mk("x_low_O", C)
        mk("wo_ready", 2)
        mk("attention_added", 1)
        for n in ("weights_loaded", "pool_setup", "dve_setup", "settled", "gate_reduced"):
            mk(n, 0)

        class Seq:

            def __init__(self, n, reg=None):
                self.n, self.reg = n, reg
                self.s = n % 2

            def __sub__(self, k):
                return Seq(self.n - k, self.reg)

            def live(self):
                return self.reg is not None or 0 <= self.n < NSEQ

        def at(name, b, k=None):
            n = per[name]
            v = b.n * n + (n if k is None else k)
            if b.reg is None:
                return max(0, min(v, NSEQ * n))
            assert v > 0, name
            return b.reg * (2 * n) + v

        def settled(eng):
            eng.sem_inc(sem["settled"], 1)

        def yhalf(s, j):
            return bank[:, (2 * s + j) % 3, :]

        def zhalf(s, j):
            return bank[:, 5 + (2 * s + j) % 3, :]

        def units(i):
            a, b = i, i - 3
            return [(k, q, e) for e in range(NEXP) for k, q in (("A", a), ("B", b)) if q.live()]

        st_a = qs[0][:, :, :].rearrange("p h s -> p (h s)").bitcast(fp32)
        st_c = qs[1][:, :, :].rearrange("p h s -> p (h s)").bitcast(fp32)
        SWO = C * 3 * D
        SG = SWO + C * D
        st_w1, st_w2 = st_a[:, 0:WKD], st_a[:, WKD:2 * WKD]
        st_qkv, st_wo, st_g = st_c[:, 0:SWO], st_c[:, SWO:SG], st_c[:, SG:SG + C * NEXP]
        BROW = (0, 32)
        st_b = [t_[r:r + 3, :, :].rearrange("p t n -> p (t n)") for r, t_ in zip(BROW, (acc["B"], xn["B"]))]
        rowsum = sb("rowsum", [P, 2, NEXP * C])
        bsum = sb("bsum", [64, 2, NEXP])
        bpart = qkp[0].rearrange("p a c s -> p a (c s)")

        def drive(eng, iteration):
            first = 4
            loops = max(NSEQ - 1 - first, 0) // 2
            for i in range(min(first, NSEQ + 3)):
                iteration(Seq(i))
            if loops:
                with eng.Fori(0, loops) as r:
                    for o in range(2):
                        iteration(Seq(first + o, r))
            for i in range(first + 2 * loops, NSEQ + 3):
                iteration(Seq(i))

        NLOAD = 8 + 6 + 2 * C + 2
        NPOOL = 9 + NEXP - 1 + 5 + 4
        NDVE = 2 * (6 + 3 * 2 + 2) + 10
        MISC_PER = 4

        block = ctx.enter_context(nc.Block())

        @block.sync
        def _(eng):
            n = [0]

            def cld(dst, src):
                n[0] += 1
                eng.dma_start(dst, src, allow_slow_non_contiguous=True).then_inc(sem["weights_loaded"], 16)

            cld(acc["A"][:, :, :], x[0, :, :].rearrange("(t p) d -> p t d", p=P))
            cld(st_w1.rearrange("p (a n) -> p a n", n=D), W1.rearrange("e (c p) n -> p (e c) n", p=P))
            cld(st_w2.rearrange("p (a n) -> p a n", n=D), W2.rearrange("e (c p) n -> p (e c) n", p=P))
            cld(st_qkv.rearrange("p (c n) -> p c n", c=C)[:, :, 0:D], Wq.rearrange("(c p) n -> p c n", p=P))
            cld(st_qkv.rearrange("p (c n) -> p c n", c=C)[:, :, D:3 * D], Wkv.rearrange("(c p) n -> p c n", p=P))
            cld(st_wo.rearrange("p (c n) -> p c n", c=C), Wo.rearrange("(c p) n -> p c n", p=P))
            cld(st_g.rearrange("p (c n) -> p c n", c=C), gate_W.rearrange("(c p) n -> p c n", p=P))
            cld(gb[:, :], gate_b.rearrange("(n o) -> n o", o=1))
            for m, b in enumerate((b1, b2)):
                for r in range(3):
                    cld(st_b[m][r:r + 1, :], b.rearrange("(o e) n -> o (e n)", o=1))
            for c in range(C):
                cld(g1c[:, :, c], g1[:, c * P:(c + 1) * P].rearrange("e p -> p e"))
                cld(be1c[:, :, c], be1[:, c * P:(c + 1) * P].rearrange("e p -> p e"))
            for dst, src in ((g2b, g2), (be2b, be2)):
                cld(dst[:, :, :].rearrange("p e n -> p (e n)"),
                    src.rearrange("(o e) n -> o (e n)", o=1).broadcast_to([P, NEXP * D]))
            assert n[0] == NLOAD, (n, NLOAD)

            def rows(t, b):
                v = t[b.n, :, :] if b.reg is None else \
                    t[bass.ds(b.reg * 2 + b.n, 1), :, :].rearrange("o s d -> (o s) d")
                return v.rearrange("(t p) d -> p t d", p=P)

            def iteration(i):
                b = i
                if b.live():
                    eng.wait_ge(sem["z_summed_A"], at("z_summed_A", b))
                    settled(eng)
                    eng.dma_start(rows(out, b), acc["A"][:, :, :]).then_inc(sem["x1_kept"], 16)
                b = i - 3
                if b.live():
                    eng.wait_ge(sem["z_summed_B"], at("z_summed_B", b))
                    settled(eng)
                    eng.dma_start(rows(out, b), acc["B"][:, :, :]).then_inc(sem["out_stored"], 16)
                b = Seq(i.n + 1, i.reg)
                if b.live():
                    eng.wait_ge(sem["x1_kept"], at("x1_kept", i))
                    settled(eng)
                    eng.wait_ge(sem["ln_ready_Q"], at("ln_ready_Q", i))
                    settled(eng)
                    eng.dma_start(acc["A"][:, :, :], rows(x, b)).then_inc(sem["x_loaded"], 16)
                b = i - 2
                if b.live():
                    eng.wait_ge(sem["x1_kept"], at("x1_kept", b))
                    settled(eng)
                    eng.wait_ge(sem["attention_added"], at("attention_added", b - 1))
                    settled(eng)
                    eng.wait_ge(sem["pv_ready"], at("pv_ready", b))
                    settled(eng)
                    eng.dma_start(res[:, :, :], rows(out, b)).then_inc(sem["x1_back"], 16)
                b = i - 1
                if b.live():
                    eng.wait_ge(sem["maxima_copied"], at("maxima_copied", b))
                    settled(eng)
                    for p in range(3):
                        eng.dma_start(qs[b.s][KR + p:KR + p + 1, :, :], nmt[p * H:(p + 1) * H, :]).then_inc(sem["maxima_placed"], 16)
                b = i
                if b.live():
                    eng.wait_ge(sem["keys_scored"], at("keys_scored", b - 2))
                    settled(eng)
                    for n_, (src, dst, parts) in enumerate(((qkp[0], qs, QPART), (qkp[1], ks, KPART))):
                        eng.wait_ge(sem["qk_part3"], at("qk_part3", b, C * (n_ + 1)))
                        settled(eng)
                        for hc in range(HC):
                            for g in range(G):
                                eng.dma_start(dst[b.s][g * HD:(g + 1) * HD, hc::HC, :],
                                                  src[hc * HD:(hc + 1) * HD, parts[g], :, :]).then_inc(sem["stacks_placed"], 16)

            drive(eng, iteration)
            eng.wait_ge(sem["out_stored"], at("out_stored", Seq(NSEQ - 1)))
            eng.wait_ge(sem["x_loaded"], at("x_loaded", Seq(NSEQ - 2)))
            eng.wait_ge(sem["stacks_placed"], at("stacks_placed", Seq(NSEQ - 1)))


        @block.gpsimd
        def _(eng):
            cp = [0]

            def step(ins):
                cp[0] += 1
                ins.then_inc(sem["pool_setup"], 1)
                eng.wait_ge(sem["pool_setup"], cp[0])

            step(eng.memset(identf[:, :], 0.0))
            step(eng.affine_select(out=identf[:, :], in_=identf[:, :], compare_op=ALU.not_equal, fill=1.0,
                                   base=0, pattern=[[-1, P]], channel_multiplier=1))
            step(eng.tensor_copy(identb[:, :], identf[:, :]))
            step(eng.memset(mask_q[:, :], 0.0))
            step(eng.affine_select(out=mask_q[:, :], in_=mask_q[:, :], compare_op=ALU.is_ge, fill=MASKED,
                                   base=0, pattern=[[-1, P]], channel_multiplier=1))
            step(eng.memset(mask_k[:, :], 0.0))
            step(eng.affine_select(out=mask_k[:, :], in_=mask_k[:, :], compare_op=ALU.is_ge, fill=MASKED,
                                   base=0, pattern=[[1, P]], channel_multiplier=-1))
            step(eng.memset(neghalf[:, :], -0.5))
            step(eng.memset(lower[:, :, :, :], 0.0))
            for e in range(NEXP):
                if e:
                    step(eng.memset(lower[:, :, e, 0:e], 1.0))
            for m, r in enumerate(BROW):
                step(eng.memset(ones3[m][:, :], 0.0))
                step(eng.memset(ones3[m][r:r + 3, :], 1.0))
            step(eng.memset(bias[:, :, :], 0.0))
            for s in range(2):
                step(eng.memset(ks[s][64:P, :, :], 1.0))
                step(eng.memset(va[s][:, :, :, HD:HD + 1], 1.0))
            assert cp[0] == NPOOL, (cp, NPOOL)

            def ln(k, b):
                eng.wait_ge(sem[f"ln_stats_{k}"], at(f"ln_stats_{k}", b))
                settled(eng)
                eng.tensor_scalar(rtmp[k][:, :], mv[k][:, :, 1], LN_EPS, None, ALU.add).then_inc(sem[f"ln_var_{k}"], 1)
                eng.wait_ge(sem[f"ln_var_{k}"], at(f"ln_var_{k}", b))
                eng.tensor_tensor(rstd[k][:, :], rtmp[k][:, :], neghalf[:, 0:T], ALU.pow).then_inc(sem[f"ln_rstd_{k}"], 1)

            def add(unit):
                k, b, e = unit
                eng.wait_ge(sem[f"z_shifted_{k}"], at(f"z_shifted_{k}", b, e + 1))
                eng.wait_ge(sem[f"z_scaled_{k}"], at(f"z_scaled_{k}", b, 2 * e + 2))
                eng.tensor_tensor(acc[k][:, :, :], acc[k][:, :, :], u[:, :, :], ALU.add).then_inc(sem[f"z_summed_{k}"], 1)

            def iteration(i):
                us = units(i)
                for s in range(len(us) + 2):
                    if s < len(us):
                        k, b, e = us[s]
                        eng.wait_ge(sem[f"y_squares_{k}"], at(f"y_squares_{k}", b, e + 1))
                        eng.wait_ge(sem[f"y_normed_{k}"], at(f"y_normed_{k}", b, 2 * e))
                        settled(eng)
                        eng.tensor_scalar(tmp1[k][:, :], ss1[k][:, :], 1.0 / D, LN_EPS, ALU.mult,
                                          ALU.add).then_inc(sem[f"y_var_{k}"], 1)
                        eng.wait_ge(sem[f"y_var_{k}"], at(f"y_var_{k}", b, e + 1))
                        eng.tensor_tensor(rs1[k][:, :], tmp1[k][:, :], neghalf[:, 0:T],
                                          ALU.pow).then_inc(sem[f"y_rstd_{k}"], 1)
                    if s >= 3:
                        add(us[s - 3])
                    if s >= 2:
                        k, b, e = us[s - 2]
                        eng.wait_ge(sem[f"z_squares_{k}"], at(f"z_squares_{k}", b, e + 1))
                        if e == 0:
                            eng.wait_ge(sem[f"gate_step_{k}"], at(f"gate_step_{k}", b))
                        settled(eng)
                        eng.tensor_scalar(tmp2[k][:, :], ss2[k][:, :], 1.0 / D, LN_EPS, ALU.mult,
                                          ALU.add).then_inc(sem[f"z_var_{k}"], 1)
                        eng.wait_ge(sem[f"z_var_{k}"], at(f"z_var_{k}", b, e + 1))
                        eng.tensor_tensor(rs2[k][:, :], tmp2[k][:, :], neghalf[:, 0:T],
                                          ALU.pow).then_inc(sem[f"z_rstd_{k}"], 1)
                        eng.wait_ge(sem[f"z_rstd_{k}"], at(f"z_rstd_{k}", b, e + 1))
                        eng.wait_ge(sem[f"z_scaled_{k}"], at(f"z_scaled_{k}", b, 2 * e))
                        eng.tensor_tensor(wst[k][:, :], rs2[k][:, :], wgt[k][:, :, e], ALU.mult).then_inc(sem[f"z_factor_{k}"], 1)
                if us:
                    add(us[-1])
                if i.live():
                    ln("Q", i)
                if (i - 2).live():
                    ln("B", i - 2)
                if Seq(i.n + 1, i.reg).live():
                    ln("A", Seq(i.n + 1, i.reg))
                if i.live():
                    for n_ in range(2 * C):
                        eng.wait_ge(sem["qk_part2"], at("qk_part2", i, n_ + 1))
                        eng.tensor_tensor(qkp[n_ // C][:, 2, n_ % C, :], qkr,
                                              qkp[n_ // C][:, 1, n_ % C, :], ALU.subtract).then_inc(sem["qk_part3"], 1)

            ln("A", Seq(0))
            drive(eng, iteration)


        @block.scalar
        def _(eng):
            def high(k, b, last=None):
                for c in range(C):
                    eng.wait_ge(sem[f"x_turned_{k}"], at(f"x_turned_{k}", b, c + 1))
                    eng.activation(xt[k][0][:, c, :], tps[:, c, :], ACT.Copy).then_inc(sem[f"x_high_{k}"], 1)

            def iteration(i):
                us = units(i)
                for s in range(len(us) + 2):
                    if s < len(us):
                        k, b, e = us[s]
                        eng.wait_ge(sem[f"y_var_{k}"], at(f"y_var_{k}", b, e))
                        if s:
                            kk, bb, ee = us[s - 1]
                            eng.wait_ge(sem[f"y_squares_{kk}"], at(f"y_squares_{kk}", bb, ee + 1))
                            if s > 2:
                                kk, bb, ee = us[s - 3]
                                eng.wait_ge(sem[f"z_squares_{kk}"], at(f"z_squares_{kk}", bb, ee + 1))
                        else:
                            for kk, bb in (("A", i - 1), ("B", i - 4)):
                                if bb.live():
                                    eng.wait_ge(sem[f"z_squares_{kk}"], at(f"z_squares_{kk}", bb))
                        for t in range(T):
                            if t % 2 == 0:
                                eng.wait_ge(sem[f"y_ready_{k}"], at(f"y_ready_{k}", b, 2 * e + t // 2 + 1))
                            ins = eng.activation(junk[:, t, :], yhalf(s, t // 2)[:, (t % 2) * D:(t % 2 + 1) * D],
                                                 ACT.Square, accum_out=ss1[k][:, t:t + 1])
                        ins.then_inc(sem[f"y_squares_{k}"], 1)
                        if e == 0:
                            eng.wait_ge(sem[f"gate_step_{k}"], at(f"gate_step_{k}", b, 2))
                            eng.activation(gexp[k][:, :, :], gcmp[:, :, 0, :], ACT.Exp).then_inc(sem[f"gate_exp_{k}"], 1)
                    if 1 <= s <= len(us):
                        k, b, e = us[s - 1]
                        if s >= 2:
                            kk, bb, ee = us[s - 2]
                            eng.wait_ge(sem[f"h_low_{kk}"], at(f"h_low_{kk}", bb, 2 * ee + 2))
                        for c in range(C):
                            eng.wait_ge(sem[f"y_turned_{k}"], at(f"y_turned_{k}", b, 2 * e + c + 1))
                            eng.activation(hf[:, c, :], tps[:, c, :], ACT.Relu,
                                               bias=be1c[:, e, c:c + 1], scale=g1c[:, e, c:c + 1]).then_inc(sem[f"h_ready_{k}"], 1)
                    if s >= 2:
                        k, b, e = us[s - 2]
                        eng.wait_ge(sem[f"z_var_{k}"], at(f"z_var_{k}", b, e))
                        if s < len(us):
                            eng.wait_ge(sem[f"y_squares_{us[s][0]}"], at(f"y_squares_{us[s][0]}", us[s][1], us[s][2] + 1))
                        else:
                            kk, bb, ee = us[s - 3] if s > 2 else us[-1]
                            eng.wait_ge(sem[f"z_squares_{kk}" if s > 2 else f"y_squares_{kk}"], at(f"z_squares_{kk}" if s > 2 else f"y_squares_{kk}", bb, ee + 1))
                            eng.wait_ge(sem[f"y_squares_{us[-1][0]}"], at(f"y_squares_{us[-1][0]}", us[-1][1]))
                        for t in range(T):
                            if t % 2 == 0:
                                eng.wait_ge(sem[f"z_ready_{k}"], at(f"z_ready_{k}", b, 2 * e + t // 2 + 1))
                            ins = eng.activation(junk[:, t, :], zhalf(s - 2, t // 2)[:, (t % 2) * D:(t % 2 + 1) * D],
                                                 ACT.Square, accum_out=ss2[k][:, t:t + 1])
                        ins.then_inc(sem[f"z_squares_{k}"], 1)
                    if 1 <= s <= len(us):
                        k, b, e = us[s - 1]
                        if s >= 2:
                            kk, bb, ee = us[s - 2]
                            eng.wait_ge(sem[f"z_ready_{kk}"], at(f"z_ready_{kk}", bb, 2 * ee + 2))
                        for c in range(C):
                            eng.activation(hh[:, c, :], tps[:, c, :], ACT.Relu,
                                           bias=be1c[:, e, c:c + 1], scale=g1c[:, e, c:c + 1]).then_inc(sem[f"h_high_{k}"], 1)
                m, e_ = i - 1, i - 2
                if e_.live():
                    for h in range(H):
                        if h == 0:
                            for k, b in (("A", i), ("B", i - 3)):
                                if b.live():
                                    eng.wait_ge(sem[f"z_summed_{k}"], at(f"z_summed_{k}", b))
                            eng.wait_ge(sem["stacks_placed"], at("stacks_placed", i - 1))
                        if h >= NPT:
                            eng.wait_ge(sem["pv_ready"], at("pv_ready", e_, (h - NPT) // QUAD + 1))
                        for p in range(2):
                            eng.wait_ge(sem["keys_scored"], at("keys_scored", e_, 2 * h + p + 1))
                            eng.activation(pt[:, h % NPT, PCOL[p]:PCOL[p + 1]], eps_[:, PCOL[p]:PCOL[p + 1]], ACT.Exp,
                                           scale=SCALE).then_inc(sem["exp_ready"], 1)
                        if h % QUAD == 1 and h >= QUAD:
                            o_copy(e_, h // QUAD - 1)
                    o_copy(e_, QUAD - 1)
                if m.live():
                    eng.wait_ge(sem["maxima_turned"], at("maxima_turned", m))
                    eng.wait_ge(sem["maxima_placed"], at("maxima_placed", m - 1))
                    eng.activation(nmt[:, :], rps.bitcast(bf16)[0:3 * H, 0:S], ACT.Copy).then_inc(sem["maxima_copied"], 1)
                nxt = Seq(i.n + 1, i.reg)
                if e_.live():
                    high("O", e_)
                if i.live():
                    high("Q", i)
                    for n_ in range(2 * C):
                        eng.wait_ge(sem["qk_ready"], at("qk_ready", i, n_ + 1))
                        if n_ == 0:
                            eng.wait_ge(sem["stacks_placed"], at("stacks_placed", i - 1))
                        eng.activation(qkp[n_ // C][:, 0, n_ % C, :], qkb[n_], ACT.Copy).then_inc(sem["qk_part1"], 1)
                        eng.wait_ge(sem["qk_rest"], at("qk_rest", i, n_ + 1))
                        eng.activation(qkp[n_ // C][:, 1, n_ % C, :], qkr, ACT.Copy).then_inc(sem["qk_part2"], 1)
                if nxt.live():
                    high("A", nxt)
                if e_.live():
                    high("B", e_)

            def o_copy(b, g):
                eng.wait_ge(sem["pv_ready"], at("pv_ready", b, g + 1))
                eng.wait_ge(sem["pv_turned"], at("pv_turned", b, g))
                eng.activation(ot[:, :], ops, ACT.Copy).then_inc(sem["pv_copied"], 1)

            high("A", Seq(0))
            drive(eng, iteration)

        @block.vector
        def _(eng):
            eng.wait_ge(sem["weights_loaded"], 16 * NLOAD)
            eng.wait_ge(sem["pool_setup"], NPOOL)
            cd = [0]

            def step(ins):
                cd[0] += 1
                ins.then_inc(sem["dve_setup"], 1)
                eng.wait_ge(sem["dve_setup"], cd[0])

            for m, (st, w) in enumerate(((st_w1, w1), (st_w2, w2))):
                v = st.rearrange("p (a n) -> p a n", n=D)
                step(eng.tensor_reduce(rowsum[:, m, :], v, AX.X, ALU.add))
                step(eng.tensor_scalar(rowsum[:, m, :], rowsum[:, m, :], -1.0 / D, None, ALU.mult))
                step(eng.tensor_tensor(v, v, rowsum[:, m, :].unsqueeze(2).broadcast_to([P, NEXP * C, D]), ALU.add))
                b = st_b[m].rearrange("p (a n) -> p a n", n=D)
                bs = bsum[BROW[m]:BROW[m] + 3, m, :]
                step(eng.tensor_reduce(bs, b, AX.X, ALU.add))
                step(eng.tensor_scalar(bs, bs, -1.0 / D, None, ALU.mult))
                step(eng.tensor_tensor(b, b, bs.unsqueeze(2).broadcast_to([3, NEXP, D]), ALU.add))
                r0 = BROW[m]
                dst = bias[r0:r0 + 3, :, :].rearrange("p e n -> p (e n)")
                bp = bpart[r0:r0 + 3, :, :]
                for r in range(3):
                    step(eng.tensor_copy(bp[:, r, :], st_b[m]))
                    if r < 2:
                        step(eng.tensor_tensor(st_b[m], st_b[m], bp[:, r, :], ALU.subtract))
                    if r == 0:
                        step(eng.tensor_scalar(dst, bp[:, 0, :], identf[r0:r0 + 3, r0:r0 + 1], None, ALU.mult))
                    else:
                        step(eng.scalar_tensor_tensor(out=dst, in0=bp[:, r, :], scalar=identf[r0:r0 + 3, r0 + r:r0 + r + 1], in1=dst,
                                                      op0=ALU.mult, op1=ALU.add))
            for st, w in ((st_w1, w1), (st_w2, w2), (st_qkv, wqkv), (st_wo, wo), (st_g, gw)):
                flat = [w_[:, :, :, :].rearrange("p e c n -> p (e c n)") if len(w_.shape) == 4 else
                        w_[:, :, :].rearrange("p c n -> p (c n)") for w_ in w]
                step(eng.tensor_copy(flat[0], st))
                step(eng.tensor_tensor(flat[1], st, flat[0].bitcast(fp32), ALU.subtract))
            assert cd[0] == NDVE, (cd, NDVE)

            def ln(k, b, src):
                for t in range(T):
                    ins = eng.bn_stats(out=st6[k][:, t, :], in_=src[:, t, :])
                ins.then_inc(sem[f"ln_parts_{k}"], 1)
                eng.wait_ge(sem[f"ln_parts_{k}"], at(f"ln_parts_{k}", b))
                settled(eng)
                for t in range(T):
                    ins = eng.bn_aggr(out=mv[k][:, t, :], in_=st6[k][:, t, :])
                ins.then_inc(sem[f"ln_stats_{k}"], 1)

            def ln_out(k, b, src):
                eng.wait_ge(sem[f"ln_rstd_{k}"], at(f"ln_rstd_{k}", b))
                for t in range(T):
                    ins = eng.tensor_scalar(xn[k][:, t, :], src[:, t, :], mv[k][:, t, 0:1], rstd[k][:, t:t + 1],
                                            ALU.subtract, ALU.mult)
                ins.then_inc(sem[f"ln_ready_{k}"], 1)

            def low(k, b):
                for c in range(C):
                    eng.wait_ge(sem[f"x_high_{k}"], at(f"x_high_{k}", b, c + 1))
                    eng.tensor_tensor(xt[k][1][:, c, :], tps[:, c, :], xt[k][0][:, c, :].bitcast(fp32),
                                          ALU.subtract).then_inc(sem[f"x_low_{k}"], 1)

            def gate(i, k, b):
                n = [0]

                def g(ins, w=True):
                    ins.then_inc(sem[f"gate_step_{k}"], 1)
                    n[0] += 1
                    if w:
                        eng.wait_ge(sem[f"gate_step_{k}"], at(f"gate_step_{k}", b, n[0]))

                eng.wait_ge(sem[f"gate_turned_{k}"], at(f"gate_turned_{k}", b))
                g(eng.tensor_copy(gs[k][:, :, :], gps[k][:, 0:T * NEXP].rearrange("p (t e) -> p t e", e=NEXP)))
                eng.tensor_reduce(gmax[k][:, :], gs[k][:, :, :], AX.X, ALU.max).then_inc(sem["gate_reduced"], 1)
                waitmisc(b)
                g(eng.tensor_tensor(gcmp[:, :, 0, :], gs[k][:, :, :],
                                    gmax[k][:, :].unsqueeze(2).broadcast_to([P, T, NEXP]), ALU.subtract), False)
                mine = gs[k][:, :, :].unsqueeze(3).broadcast_to([P, T, NEXP, NEXP])
                other = gs[k][:, :, :].unsqueeze(2).broadcast_to([P, T, NEXP, NEXP])
                eng.wait_ge(sem[f"gate_exp_{k}"], at(f"gate_exp_{k}", b))
                g(eng.tensor_tensor(gcmp[:, :, :, :], other, mine, ALU.is_gt))
                g(eng.tensor_tensor(gcmq[:, :, :, :], other, mine, ALU.is_equal))
                g(eng.tensor_tensor(gcmq[:, :, :, :], gcmq[:, :, :, :], lower[:, :, :, :], ALU.mult))
                g(eng.tensor_tensor(gcmp[:, :, :, :], gcmp[:, :, :, :], gcmq[:, :, :, :], ALU.add))
                g(eng.tensor_reduce(grank[k][:, :, :], gcmp[:, :, :, :], AX.X, ALU.add))
                g(eng.scalar_tensor_tensor(out=gexp[k][:, :, :], in0=grank[k][:, :, :], scalar=1.5,
                                           in1=gexp[k][:, :, :], op0=ALU.is_lt, op1=ALU.mult))
                eng.tensor_reduce(gsum[k][:, :], gexp[k][:, :, :], AX.X, ALU.add).then_inc(sem["gate_reduced"], 1)
                waitmisc(b)
                g(eng.reciprocal(gsum[k][:, :], gsum[k][:, :]))
                g(eng.scalar_tensor_tensor(out=wgt[k][:, :, :], in0=gexp[k][:, :, :], scalar=0.5,
                                           in1=gsum[k][:, :].unsqueeze(2).broadcast_to([P, T, NEXP]),
                                           op0=ALU.mult, op1=ALU.mult))
                assert n[0] == per[f"gate_step_{k}"]

            misc = {"n": 0, "reg": None, "per": 0}

            def waitmisc(b):
                misc["n"] += 1
                v = misc["n"]
                if misc["reg"] is None:
                    eng.wait_ge(sem["gate_reduced"], v)
                else:
                    eng.wait_ge(sem["gate_reduced"], misc["reg"] * misc["per"] + v)

            def iteration(i):
                if i.reg is None and misc["reg"] is not None:
                    misc["n"] += misc["per"] * (misc["loops"] - 1)
                    misc["reg"] = None
                if i.reg is not None:
                    misc["reg"], misc["per"], misc["loops"] = i.reg, 2 * MISC_PER, (NSEQ - 5) // 2
                us = units(i)
                for k, b in (("A", i), ("B", i - 3)):
                    if b.live():
                        eng.scalar_tensor_tensor(out=acc[k][:, :, :], in0=xn[k][:, :, :], scalar=0.5,
                                                     in1=acc[k][:, :, :], op0=ALU.mult, op1=ALU.add).then_inc(sem[f"sum_begun_{k}"], 1)
                        if k == "A" and (i - 1).live():
                            eng.wait_ge(sem["qk_part3"], at("qk_part3", i - 1))
                        eng.wait_ge(sem[f"gate_ready_{k}"], at(f"gate_ready_{k}", b))
                        eng.tensor_scalar(gt[k], gps[k][0:NEXP, :], gb[:, 0:1], None, ALU.add).then_inc(sem[f"gate_biased_{k}"], 1)
                for s in range(len(us) + 2):
                    if s < len(us):
                        k, b, e = us[s]
                        if e == 0:
                            gate(i, k, b)
                        eng.wait_ge(sem[f"y_rstd_{k}"], at(f"y_rstd_{k}", b, e + 1))
                        if s:
                            kk, bb, ee = us[s - 1]
                            eng.wait_ge(sem[f"y_turned_{kk}"], at(f"y_turned_{kk}", bb, 2 * ee + 2))
                        for j in range(2):
                            y = yhalf(s, j).rearrange("p (t n) -> p t n", t=2)
                            eng.tensor_tensor(yn[:, 2 * j:2 * j + 2, :], y,
                                                  rs1[k][:, 2 * j:2 * j + 2].unsqueeze(2).broadcast_to([P, 2, D]),
                                                  ALU.mult).then_inc(sem[f"y_normed_{k}"], 1)
                    if 1 <= s <= len(us):
                        k, b, e = us[s - 1]
                        if s >= 2:
                            kk, bb, ee = us[s - 2]
                            eng.wait_ge(sem[f"z_ready_{kk}"], at(f"z_ready_{kk}", bb, 2 * ee + 2))
                        for c in range(C):
                            eng.wait_ge(sem[f"h_ready_{k}"], at(f"h_ready_{k}", b, 2 * e + c + 1))
                            eng.wait_ge(sem[f"h_high_{k}"], at(f"h_high_{k}", b, 2 * e + c + 1))
                            eng.tensor_tensor(hl[:, c, :], hf[:, c, :], hh[:, c, :].bitcast(fp32),
                                              ALU.subtract).then_inc(sem[f"h_low_{k}"], 1)
                    if s >= 2:
                        k, b, e = us[s - 2]
                        eng.wait_ge(sem[f"z_factor_{k}"], at(f"z_factor_{k}", b, e + 1))
                        if s >= 3:
                            kk, bb, ee = us[s - 3]
                            eng.wait_ge(sem[f"z_summed_{kk}"], at(f"z_summed_{kk}", bb, ee + 1))
                        for t in range(T):
                            ins = eng.scalar_tensor_tensor(
                                out=u[:, t, :], in0=zhalf(s - 2, t // 2)[:, (t % 2) * D:(t % 2 + 1) * D],
                                scalar=wst[k][:, t:t + 1], in1=g2b[:, e, :], op0=ALU.mult, op1=ALU.mult)
                            if t % 2:
                                ins.then_inc(sem[f"z_scaled_{k}"], 1)
                    if s >= 2:
                        k, b, e = us[s - 2]
                        if e == 0:
                            eng.wait_ge(sem[f"sum_begun_{k}"], at(f"sum_begun_{k}", b))
                        else:
                            eng.wait_ge(sem[f"z_summed_{k}"], at(f"z_summed_{k}", b, e))
                        for t in range(T):
                            ins = eng.scalar_tensor_tensor(
                                out=acc[k][:, t, :], in0=be2b[:, e, :], scalar=wgt[k][:, t, e:e + 1], in1=acc[k][:, t, :],
                                op0=ALU.mult, op1=ALU.add)
                        ins.then_inc(sem[f"z_shifted_{k}"], 1)
                nxt = Seq(i.n + 1, i.reg)
                if i.live():
                    eng.wait_ge(sem["z_summed_A"], at("z_summed_A", i))
                    ln("Q", i, acc["A"])
                    ln_out("Q", i, acc["A"])
                m, e_ = i - 1, i - 2
                for h in range(H):
                    if m.live():
                        for p in range(2):
                            eng.wait_ge(sem["queries_scored"], at("queries_scored", m, 2 * h + p + 1))
                            eng.tensor_reduce(bm[:, h, PCOL[p] // P:PCOL[p + 1] // P],
                                              mps[:, PCOL[p]:PCOL[p + 1]].rearrange("p (b n) -> p b n", n=P),
                                              AX.X, ALU.max).then_inc(sem["block_maxima"], 1)
                    if e_.live() and h % QUAD == QUAD - 1 and h >= QUAD:
                        normalise(e_, h // QUAD - 1)
                if m.live():
                    eng.wait_ge(sem["block_maxima"], at("block_maxima", m))
                    for t in range(T):
                        o = MCOL[t] // P
                        ins = eng.tensor_reduce(nm[:, t, :], bm[:, :, o:o + t + 1], AX.X, ALU.max, negate=True)
                    ins.then_inc(sem["maxima_ready"], 1)
                    eng.wait_ge(sem["maxima_ready"], at("maxima_ready", m))
                    eng.wait_ge(sem["maxima_turned"], at("maxima_turned", m - 1))
                    src = nm
                    for p in range(3):
                        eng.tensor_copy(nmp[:, :, p, :], src[:, :, :]).then_inc(sem["maxima_part"], 1)
                        if p < 2:
                            eng.wait_ge(sem["maxima_part"], at("maxima_part", m, p + 1))
                            eng.tensor_tensor(nmr[:, :, :], src[:, :, :], nmp[:, :, p, :], ALU.subtract).then_inc(sem["maxima_rest"], 1)
                            eng.wait_ge(sem["maxima_rest"], at("maxima_rest", m, p + 1))
                        src = nmr
                if e_.live():
                    normalise(e_, QUAD - 1)
                if e_.live():
                    low("O", e_)
                if i.live():
                    low("Q", i)
                if e_.live():
                    eng.wait_ge(sem["x1_back"], at("x1_back", e_))
                    eng.wait_ge(sem["out_stored"], at("out_stored", e_ - 1))
                    for j in range(2):
                        eng.wait_ge(sem["wo_ready"], at("wo_ready", e_, j + 1))
                        ins = eng.tensor_tensor(acc["B"][:, 2 * j:2 * j + 2, :],
                                                bank[:, 6 + j, :].rearrange("p (t n) -> p t n", t=2),
                                                res[:, 2 * j:2 * j + 2, :], ALU.add)
                    ins.then_inc(sem["attention_added"], 1)
                    eng.wait_ge(sem["attention_added"], at("attention_added", e_))
                    ln("B", e_, acc["B"])
                if nxt.live():
                    eng.wait_ge(sem["x_loaded"], at("x_loaded", i))
                    ln("A", nxt, acc["A"])
                if i.live():
                    for n_ in range(2 * C):
                        eng.wait_ge(sem["qk_part1"], at("qk_part1", i, n_ + 1))
                        if n_:
                            eng.wait_ge(sem["qk_part3"], at("qk_part3", i, n_))
                        eng.tensor_tensor(qkr, qkb[n_], qkp[n_ // C][:, 0, n_ % C, :],
                                              ALU.subtract).then_inc(sem["qk_rest"], 1)
                    for j in range(2):
                        eng.wait_ge(sem["v_ready"], at("v_ready", i, j + 1))
                        eng.tensor_copy(va[i.s][:, 2 * j:2 * j + 2, :, 0:HD],
                                            bank[:, 6 + j, :].rearrange("p (t h d) -> p t h d", t=2, h=H)).then_inc(sem["v_copied"], 1)
                if e_.live():
                    if i.live():
                        eng.wait_ge(sem["x_turned_Q"], at("x_turned_Q", i))
                    ln_out("B", e_, acc["B"])
                if nxt.live():
                    if e_.live():
                        eng.wait_ge(sem["x_turned_O"], at("x_turned_O", e_))
                    ln_out("A", nxt, acc["A"])
                    low("A", nxt)
                if e_.live():
                    low("B", e_)

            def normalise(b, g):
                if g == 0:
                    eng.wait_ge(sem["x_turned_O"], at("x_turned_O", b - 1))
                    if (b - (-2)).live():
                        eng.wait_ge(sem["x_turned_A"], at("x_turned_A", b - (-2)))
                eng.wait_ge(sem["pv_turned"], at("pv_turned", b, g + 1))
                v = rps.rearrange("p (t q d) -> p t q d", t=T, q=QUAD)
                eng.reciprocal(rden[:, :, :], v[:, :, :, HD]).then_inc(sem["sums_inverted"], 1)
                eng.wait_ge(sem["sums_inverted"], at("sums_inverted", b, g + 1))
                eng.tensor_tensor(on[:, :, g * QUAD * HD:(g + 1) * QUAD * HD].rearrange("p t (q d) -> p t q d", q=QUAD),
                                      v[:, :, :, 0:HD], rden[:, :, :].unsqueeze(3).broadcast_to([P, T, QUAD, HD]),
                                      ALU.mult).then_inc(sem["pv_normed"], 1)

            ln("A", Seq(0), acc["A"])
            ln_out("A", Seq(0), acc["A"])
            low("A", Seq(0))
            drive(eng, iteration)


        @block.tensor
        def _(eng):
            eng.wait_ge(sem["pool_setup"], NPOOL)
            eng.wait_ge(sem["dve_setup"], NDVE)
            PROD = ((0, 0), (0, 1), (1, 0))

            def xpose(k, b):
                eng.wait_ge(sem[f"ln_ready_{k}"], at(f"ln_ready_{k}", b))
                for c in range(C):
                    for t in range(T):
                        mm = eng.transpose(tps[:, c, t * P:(t + 1) * P], xn[k][:, t, c * P:(c + 1) * P], identf[:, :])
                    mm.then_inc(sem[f"x_turned_{k}"], 1)

            def tokens(out_, lhs, rhs, m=None, e=None):
                n = 0
                for c in range(C):
                    for a, w in PROD:
                        n += 1
                        mm = eng.matmul(out_, lhs(a, c), rhs(w, c), start=(n == 1),
                                        stop=(n == 3 * C and m is None))
                if m is not None:
                    mm = eng.matmul(out_, ones3[m][:, :], bias[:, e, :], start=False, stop=True)
                return mm

            def iteration(i):
                us = units(i)
                for k, b in (("A", i), ("B", i - 3)):
                    if not b.live():
                        continue
                    eng.wait_ge(sem[f"x_low_{k}"], at(f"x_low_{k}", b))
                    n = 0
                    for c in range(C):
                        for a, w in PROD:
                            n += 1
                            mm = eng.matmul(gps[k][0:NEXP, :], gw[w][:, c, :], xt[k][a][:, c, :], start=(n == 1),
                                            stop=(n == 3 * C))
                    mm.then_inc(sem[f"gate_ready_{k}"], 1)
                for s in range(len(us) + 2):
                    if s < len(us):
                        k, b, e = us[s]
                        for t in range(T):
                            if t % 2 == 0 and 2 * s + t // 2 >= 3:
                                kk, bb, ee = us[(2 * s + t // 2 - 3) // 2]
                                v = 2 * ee + (2 * s + t // 2 - 3) % 2 + 1
                                eng.wait_ge(sem[f"y_normed_{kk}"], at(f"y_normed_{kk}", bb, v))
                            mm = tokens(yhalf(s, t // 2)[:, (t % 2) * D:(t % 2 + 1) * D],
                                        lambda a, c: xt[k][a][:, c, t * P:(t + 1) * P],
                                        lambda w, c: w1[w][:, e, c, :], 0, e)
                            if t % 2:
                                mm.then_inc(sem[f"y_ready_{k}"], 1)
                        if e == 0:
                            eng.wait_ge(sem[f"gate_biased_{k}"], at(f"gate_biased_{k}", b))
                            settled(eng)
                            for t in range(T):
                                mm = eng.transpose(gps[k][:, t * NEXP:(t + 1) * NEXP], gt[k][:, t * P:(t + 1) * P],
                                                   identf[0:NEXP, 0:NEXP])
                            mm.then_inc(sem[f"gate_turned_{k}"], 1)
                    if 1 <= s <= len(us):
                        k, b, e = us[s - 1]
                        eng.wait_ge(sem[f"y_normed_{k}"], at(f"y_normed_{k}", b, 2 * e + 2))
                        if s >= 2:
                            kk, bb, ee = us[s - 2]
                            eng.wait_ge(sem[f"h_high_{kk}"], at(f"h_high_{kk}", bb, 2 * ee + 2))
                        for c in range(C):
                            for t in range(T):
                                mm = eng.transpose(tps[:, c, t * P:(t + 1) * P], yn[:, t, c * P:(c + 1) * P],
                                                   identf[:, :])
                            mm.then_inc(sem[f"y_turned_{k}"], 1)
                    if s >= 2:
                        k, b, e = us[s - 2]
                        eng.wait_ge(sem[f"h_low_{k}"], at(f"h_low_{k}", b, 2 * e + 2))
                        if s == 2:
                            for kk, bb in (("A", i), ("B", i - 3)):
                                if bb.live():
                                    eng.wait_ge(sem[f"gate_step_{kk}"], at(f"gate_step_{kk}", bb, 1))
                        hp = (hh, hl)
                        for t in range(T):
                            if t % 2 == 0 and 2 * (s - 2) + t // 2 >= 3:
                                kk, bb, ee = us[(2 * (s - 2) + t // 2 - 3) // 2]
                                v = 2 * ee + (2 * (s - 2) + t // 2 - 3) % 2 + 1
                                eng.wait_ge(sem[f"z_scaled_{kk}"], at(f"z_scaled_{kk}", bb, v))
                            mm = tokens(zhalf(s - 2, t // 2)[:, (t % 2) * D:(t % 2 + 1) * D],
                                        lambda a, c: hp[a][:, c, t * P:(t + 1) * P],
                                        lambda w, c: w2[w][:, e, c, :], 1, e)
                            if t % 2:
                                mm.then_inc(sem[f"z_ready_{k}"], 1)
                m, e_ = i - 1, i - 2
                for k, b, e in us[-2:]:
                    eng.wait_ge(sem[f"y_normed_{k}"], at(f"y_normed_{k}", b))
                    eng.wait_ge(sem[f"z_scaled_{k}"], at(f"z_scaled_{k}", b))
                if m.live():
                    eng.wait_ge(sem["stacks_placed"], at("stacks_placed", m))
                for h in range(H):
                    for p in range(2):
                        if m.live():
                            if h:
                                eng.wait_ge(sem["block_maxima"], at("block_maxima", m, 2 * h - 1 + p))
                            for t in MPART[p]:
                                o = MCOL[t]
                                w_ = (t + 1) * P
                                eng.matmul(mps[:, o:o + w_], qs[m.s][0:KR, h, t * P:(t + 1) * P], ks[m.s][0:KR, h, 0:w_],
                                           start=True, stop=False)
                                mm = eng.matmul(mps[:, o + w_ - P:o + w_], identb[:, :], mask_q[:, :], start=False,
                                                stop=True)
                            mm.then_inc(sem["queries_scored"], 1)
                        if e_.live():
                            if h:
                                eng.wait_ge(sem["exp_ready"], at("exp_ready", e_, 2 * h - 1 + p))
                            elif p == 0:
                                eng.wait_ge(sem["maxima_placed"], at("maxima_placed", e_))
                                eng.wait_ge(sem["v_copied"], at("v_copied", e_))
                            for j in EPART[p]:
                                o = ECOL[j]
                                w_ = S - j * P
                                eng.matmul(eps_[:, o:o + w_], ks[e_.s][0:KR + 3, h, j * P:(j + 1) * P],
                                           qs[e_.s][0:KR + 3, h, j * P:S], start=True, stop=False)
                                mm = eng.matmul(eps_[:, o:o + P], identb[:, :], mask_k[:, :], start=False, stop=True)
                            mm.then_inc(sem["keys_scored"], 1)
                    if e_.live():
                        if h % QUAD == 0 and h >= QUAD:
                            pv(e_, h // QUAD - 1)
                        if h % QUAD == 2 and h >= QUAD:
                            o_back(e_, h // QUAD - 1)
                if e_.live():
                    pv(e_, QUAD - 1)
                    o_back(e_, QUAD - 1)
                if m.live():
                    eng.wait_ge(sem["maxima_part"], at("maxima_part", m))
                    if e_.live():
                        eng.wait_ge(sem["pv_normed"], at("pv_normed", e_))
                    settled(eng)
                    r16 = rps.bitcast(bf16)
                    for t in range(T):
                        mm = eng.transpose(r16[0:3 * H, t * P:(t + 1) * P],
                                           nmp[:, t, :, :].rearrange("p a h -> p (a h)"), identb[:, :])
                    mm.then_inc(sem["maxima_turned"], 1)
                nxt = Seq(i.n + 1, i.reg)
                if e_.live():
                    eng.wait_ge(sem["exp_ready"], at("exp_ready", e_))
                    eng.wait_ge(sem["pv_normed"], at("pv_normed", e_))
                    for c in range(C):
                        for t in range(T):
                            mm = eng.transpose(tps[:, c, t * P:(t + 1) * P], on[:, t, c * P:(c + 1) * P], identf[:, :])
                        mm.then_inc(sem["x_turned_O"], 1)
                if i.live():
                    if e_.live():
                        eng.wait_ge(sem["x_low_O"], at("x_low_O", e_))
                    xpose("Q", i)
                if m.live():
                    eng.wait_ge(sem["maxima_copied"], at("maxima_copied", m))
                if e_.live():
                    eng.wait_ge(sem["x_low_O"], at("x_low_O", e_))
                    eng.wait_ge(sem["pv_copied"], at("pv_copied", e_))
                    for t in range(T):
                        mm = tokens(bank[:, 6 + t // 2, (t % 2) * D:(t % 2 + 1) * D],
                                    lambda a, c: xt["O"][a][:, c, t * P:(t + 1) * P], lambda w, c: wo[w][:, c, :])
                        if t % 2:
                            mm.then_inc(sem["wo_ready"], 1)
                if i.live():
                    eng.wait_ge(sem["x_low_Q"], at("x_low_Q", i))
                    if m.live():
                        eng.wait_ge(sem["block_maxima"], at("block_maxima", m))
                    for n_ in range(2 * C):
                        n = 0
                        for c in range(C):
                            for a, w in PROD:
                                n += 1
                                mm = eng.matmul(qkb[n_], wqkv[w][:, c, n_ * P:(n_ + 1) * P],
                                                xt["Q"][a][:, c, :], start=(n == 1), stop=(n == 3 * C))
                        mm.then_inc(sem["qk_ready"], 1)
                    if e_.live():
                        eng.wait_ge(sem["attention_added"], at("attention_added", e_))
                    for t in range(T):
                        mm = tokens(bank[:, 6 + t // 2, (t % 2) * D:(t % 2 + 1) * D],
                                    lambda a, c: xt["Q"][a][:, c, t * P:(t + 1) * P],
                                    lambda w, c: wqkv[w][:, c, 2 * D:3 * D])
                        if t % 2:
                            mm.then_inc(sem["v_ready"], 1)
                if nxt.live():
                    xpose("A", nxt)
                if e_.live():
                    if nxt.live():
                        eng.wait_ge(sem["x_low_A"], at("x_low_A", nxt))
                    xpose("B", e_)
                if i.live():
                    eng.wait_ge(sem["qk_rest"], at("qk_rest", i))
                    eng.wait_ge(sem["v_copied"], at("v_copied", i))

            def pv(b, g):
                eng.wait_ge(sem["exp_ready"], at("exp_ready", b, 2 * (g + 1) * QUAD))
                if g:
                    eng.wait_ge(sem["pv_copied"], at("pv_copied", b, g))
                for j in range(T):
                    for q in range(QUAD):
                        h = g * QUAD + q
                        mm = eng.matmul(ops[q * 32:q * 32 + HD + 1, j * P:S], va[b.s][:, j, h, :],
                                        pt[:, h % NPT, ECOL[j]:ECOL[j] + S - j * P],
                                        start=(j == 0), stop=(j == T - 1))
                mm.then_inc(sem["pv_ready"], 1)

            def o_back(b, g):
                eng.wait_ge(sem["pv_copied"], at("pv_copied", b, g + 1))
                if g:
                    eng.wait_ge(sem["pv_normed"], at("pv_normed", b, g))
                for t in range(T):
                    mm = eng.transpose(rps[:, t * P:(t + 1) * P], ot[:, t * P:(t + 1) * P], identf[:, :])
                mm.then_inc(sem["pv_turned"], 1)

            xpose("A", Seq(0))
            drive(eng, iteration)


_INS = ['L0_attn_x', 'L0_attn_Wq', 'L0_attn_Wkv', 'L0_attn_Wo', 'L0_ffn_gate_W', 'L0_ffn_gate_b', 'L0_ffn_W1',
        'L0_ffn_b1', 'L0_ffn_g1', 'L0_ffn_be1', 'L0_ffn_W2', 'L0_ffn_b2', 'L0_ffn_g2', 'L0_ffn_be2']


def kernel(**inputs):
    import numpy as _np
    import concourse.bacc as _bacc
    from concourse import mybir as _mybir
    from concourse.bass_utils import run_bass_kernel_spmd as _run

    nc = _bacc.Bacc("TRN2", target_bir_lowering=False, num_devices=1)
    arrays, args = {}, []
    for name in _INS:
        a = _np.ascontiguousarray(inputs[name])
        arrays[f"in_{name}_dram"] = a
        args.append(nc.dram_tensor(f"in_{name}_dram", a.shape, _mybir.dt.from_np(a.dtype), kind="ExternalInput").ap())
    shape = inputs['L0_attn_x'].shape
    args.append(nc.dram_tensor("out_0_dram", shape, _mybir.dt.float32, kind="ExternalOutput").ap())
    macaron_kernel(nc, *args)
    r = _run(nc, [arrays], core_ids=[0])
    return r.results[0]["out_0_dram"]
```

```python
import concourse.bass as bass
from concourse import mybir
from contextlib import ExitStack


def macaron_kernel(nc, x, Wq, Wkv, Wo, gate_W, gate_b, W1, b1, g1, be1, W2, b2, g2, be2, out):
    fp32, fp32r, bf16 = mybir.dt.float32, mybir.dt.float32r, mybir.dt.bfloat16
    ALU, ACT, AX = mybir.AluOpType, mybir.ActivationFunctionType, mybir.AxisListType

    NSEQ, S, D = x.shape
    NEXP = gate_W.shape[1]
    P = 128
    H, HD = 16, D // 16
    T = S // P
    C = D // P
    HC = H // C
    QUAD = 4
    SCALE = float(HD) ** -0.5
    LN_EPS = 1e-5
    MASKED = -1e30
    NBLK = T * (T + 1) // 2
    WIDE = NBLK * P
    QPART = (0, 0, 0, 1, 1, 2)
    KPART = (0, 1, 2, 0, 1, 0)
    G = len(QPART)
    KR = G * HD
    MCOL = {3: 0, 2: 4 * P, 0: 7 * P, 1: 8 * P}
    ECOL = {0: 0, 1: 4 * P, 3: 7 * P, 2: 8 * P}

    MPART = ((3,), (2, 0, 1))
    EPART = ((0,), (1, 3, 2))
    PCOL = (0, T * P, WIDE)
    LEAD = 2

    ctx = ExitStack()
    with ctx:
        def sb(name, shape, dt=fp32):
            return ctx.enter_context(nc.sbuf_tensor(name, shape, dt))

        def ps(name, shape, dt=fp32):
            return ctx.enter_context(nc.psum_tensor(name, shape, dt))

        WKD = NEXP * C * D
        w1 = [sb(f"w1_{p}", [P, NEXP, C, D], fp32r) for p in "hl"]
        w2 = [sb(f"w2_{p}", [P, NEXP, C, D], fp32r) for p in "hl"]
        wqkv = [sb(f"wqkv_{p}", [P, C, 3 * D], fp32r) for p in "hl"]
        wo = [sb(f"wo_{p}", [P, C, D], fp32r) for p in "hl"]
        gw = [sb(f"gw_{p}", [P, C, NEXP], fp32r) for p in "hl"]
        gb = sb("gb", [NEXP, 1])
        bias = sb("bias", [P, NEXP, D], bf16)
        ones3 = [sb(f"ones3_{m}", [P, P], bf16) for m in range(2)]
        g1c = sb("g1c", [P, NEXP, C])
        be1c = sb("be1c", [P, NEXP, C])
        g2b = sb("g2b", [P, NEXP, D])
        be2b = sb("be2b", [P, NEXP, D])
        identf = sb("identf", [P, P])
        identb = sb("identb", [P, P], bf16)
        mask_q = sb("mask_q", [P, P], bf16)
        mask_k = sb("mask_k", [P, P], bf16)
        neghalf = sb("neghalf", [P, 2 * T])
        lower = sb("lower", [P, T, NEXP, NEXP])
        acc = {k: sb(f"z_summed_{k}", [P, T, D]) for k in "AB"}
        xhat = sb("xhat", [P, T, D])
        on = sb("on", [P, T, D])
        xt = {k: [sb(f"xt{k}_{p}", [P, C, S], fp32r) for p in "hl"] for k in "AB"}
        xt["Q"], xt["O"] = xt["A"], xt["B"]
        mv = {k: sb(f"mv{k}", [P, T, 2]) for k in "ABQ"}
        st6 = {k: sb(f"st6{k}", [P, T, 6]) for k in "ABQ"}
        rstd = {k: sb(f"rstd{k}", [P, T]) for k in "ABQ"}
        rtmp = {k: sb(f"rtmp{k}", [P, T]) for k in "ABQ"}
        gs = {k: sb(f"gs{k}", [P, T, NEXP]) for k in "AB"}
        gmax = {k: sb(f"gmax{k}", [P, T]) for k in "AB"}
        gcmp = sb("gcmp", [P, T, NEXP, NEXP])
        gcmq = sb("gcmq", [P, T, NEXP, NEXP])
        grank = {k: sb(f"grank{k}", [P, T, NEXP]) for k in "AB"}
        gexp = {k: sb(f"gexp{k}", [P, T, NEXP]) for k in "AB"}
        gsum = {k: sb(f"gsum{k}", [P, T]) for k in "AB"}
        wgt = {k: sb(f"wgt{k}", [P, T, NEXP]) for k in "AB"}
        ss1 = {k: sb(f"ss1{k}", [P, T]) for k in "AB"}
        ss2 = {k: sb(f"ss2{k}", [P, T]) for k in "AB"}
        rs1 = {k: sb(f"rs1{k}", [P, T]) for k in "AB"}
        rs2 = {k: sb(f"rs2{k}", [P, T]) for k in "AB"}
        tmp1 = {k: sb(f"tmp1{k}", [P, T]) for k in "AB"}
        tmp2 = {k: sb(f"tmp2{k}", [P, T]) for k in "AB"}
        wst = {k: sb(f"wst{k}", [P, T]) for k in "AB"}
        junk = sb("junk", [P, T, D], bf16)
        hh = sb("hh", [P, C, S], fp32r)
        hl = sb("hl", [P, C, S], fp32r)
        qs = [sb(f"qs{s}", [P, H, S], bf16) for s in range(2)]
        ks = [sb(f"ks{s}", [P, H, S], bf16) for s in range(2)]
        va = [sb(f"va{s}", [P, T, H, HD + 1]) for s in range(2)]
        bm = sb("bm", [P, H, NBLK])
        nm = sb("nm", [P, T, H])
        nmr = sb("nmr", [P, T, H])
        nmp = sb("nmp", [P, T, 3, H], bf16)
        nmt = sb("nmt", [3 * H, S], bf16)
        ot = sb("ot", [P, S])
        rden = sb("rden", [P, T, QUAD])
        NPT = 5
        O_HF = T * D
        O_U = O_HF + C * S
        O_QK = O_U + T * D
        N_QK = 3 * C * S // 2
        O_G = O_QK + 2 * N_QK
        space = sb("space", [P, max(O_G + S, NPT * WIDE)])
        pt = space[:, 0:NPT * WIDE].rearrange("p (a n) -> p a n", a=NPT)
        yn = space[:, 0:O_HF].rearrange("p (t n) -> p t n", t=T)
        hf = space[:, O_HF:O_U].rearrange("p (c n) -> p c n", c=C)
        qkr = hf
        u = space[:, O_U:O_QK].rearrange("p (t n) -> p t n", t=T)
        res = u
        qkp = [space[:, O_QK + n * N_QK:O_QK + (n + 1) * N_QK].bitcast(bf16).rearrange(
            "p (a c s) -> p a c s", a=3, c=C) for n in range(2)]
        gt = space[0:NEXP, O_G:O_G + S]

        scratch = nc.dram_tensor("scratch", [2, 3, C, P, S], bf16, kind="Internal").ap()

        bank = ps("bank", [P, 8, 512])
        tps = bank[:, 3:5, :]
        mps = bank[:, 0:3, :].rearrange("p b n -> p (b n)")
        eps_ = bank[:, 3:6, :].rearrange("p b n -> p (b n)")
        ops = bank[:, 6, :]
        rps = bank[:, 7, :]
        qkb = [bank[:, n, :] for n in (0, 1, 2, 5)]

        per = {}
        sem = {}

        def mk(name, n):
            per[name] = n
            sem[name] = ctx.enter_context(nc.semaphore(name))

        for k in "AB":
            mk(f"y_ready_{k}", 2 * NEXP)
            mk(f"y_squares_{k}", NEXP)
            mk(f"y_var_{k}", NEXP)
            mk(f"y_rstd_{k}", NEXP)
            mk(f"y_normed_{k}", 2 * NEXP)
            mk(f"y_turned_{k}", 2 * NEXP)
            mk(f"h_ready_{k}", 2 * NEXP)
            mk(f"h_high_{k}", 2 * NEXP)
            mk(f"h_low_{k}", 2 * NEXP)
            mk(f"z_ready_{k}", 2 * NEXP)
            mk(f"z_squares_{k}", NEXP)
            mk(f"z_var_{k}", NEXP)
            mk(f"z_rstd_{k}", NEXP)
            mk(f"z_factor_{k}", NEXP)
            mk(f"z_scaled_{k}", 2 * NEXP)
            mk(f"z_shifted_{k}", NEXP)
            mk(f"z_summed_{k}", NEXP)
            mk(f"sum_begun_{k}", 1)
            mk(f"gate_ready_{k}", 1)
            mk(f"gate_biased_{k}", 1)
            mk(f"gate_turned_{k}", 1)
            mk(f"gate_step_{k}", 10)
            mk(f"gate_exp_{k}", 1)
        for k in "ABQ":
            mk(f"ln_stats_{k}", 1)
            mk(f"ln_parts_{k}", 1)
            mk(f"ln_var_{k}", 1)
            mk(f"ln_rstd_{k}", 1)
            mk(f"ln_ready_{k}", 1)
            mk(f"x_turned_{k}", C)
            mk(f"x_high_{k}", C)
            mk(f"x_low_{k}", C)
        mk("x_loaded", 16)
        mk("out_stored", 16)
        mk("x1_kept", 16)
        mk("x1_back", 16)
        mk("qk_ready", 2 * C)
        mk("qk_part1", 2 * C)
        mk("qk_rest", 2 * C)
        mk("qk_part2", 2 * C)
        mk("qk_part3", 2 * C)
        mk("v_ready", 2)
        mk("v_copied", 2)
        mk("parts_stored", 16 * 2)
        mk("stacks_placed", 16 * 2 * G)
        mk("queries_scored", 2 * H)
        mk("block_maxima", 2 * H)
        mk("maxima_ready", 1)
        mk("maxima_part", 3)
        mk("maxima_rest", 2)
        mk("maxima_turned", 1)
        mk("maxima_copied", 1)
        mk("maxima_placed", 16 * 3)
        mk("keys_scored", 2 * H)
        mk("exp_ready", 2 * H)
        mk("pv_ready", QUAD)
        mk("pv_copied", QUAD)
        mk("pv_turned", QUAD)
        mk("sums_inverted", QUAD)
        mk("pv_normed", QUAD)
        mk("x_turned_O", C)
        mk("x_high_O", C)
        mk("x_low_O", C)
        mk("wo_ready", 2)
        mk("attention_added", 1)
        for n in ("weights_loaded", "pool_setup", "dve_setup", "settled", "gate_reduced"):
            mk(n, 0)

        class Seq:

            def __init__(self, n, reg=None):
                self.n, self.reg = n, reg
                self.s = n % 2

            def __sub__(self, k):
                return Seq(self.n - k, self.reg)

            def live(self):
                return self.reg is not None or 0 <= self.n < NSEQ

        def at(name, b, k=None):
            n = per[name]
            v = b.n * n + (n if k is None else k)
            if b.reg is None:
                return max(0, min(v, NSEQ * n))
            assert v > 0, name
            return b.reg * (2 * n) + v

        def settled(eng):
            eng.sem_inc(sem["settled"], 1)

        def units(i):
            return [(k, q, e) for k, q in (("A", i), ("B", i - 3)) if q.live() for e in range(NEXP)]

        def yhalf(s, j):
            return bank[:, (2 * s + j) % 3, :]

        def rotation(i):
            a, b = i, i - 3
            order = []
            if a.live():
                order.append((("gate", "A"), ("gate_step_A", a, 1)))
            if b.live():
                order += [(("wo", j), ("attention_added", b, 1)) for j in range(2)]
                order += [(("x", c), ("x_low_B", b, c + 1)) for c in range(C)]
            if b.live() and not a.live():
                order.append((("gate", "B"), ("gate_step_B", b, 1)))
            for s, (k, q, e) in enumerate(units(i)):
                order += [(("z", s, j), (f"z_scaled_{k}", q, 2 * e + j + 1)) for j in range(2)]
                if s == 0 and a.live() and b.live():
                    order.append((("gate", "B"), ("gate_step_B", b, 1)))
            return order

        def place(i, *user):
            order = rotation(i)
            n = [u_ for u_, _ in order].index(user)
            return bank[:, 5 + n % 3, :], (order[n - 3][1] if n >= 3 else None)

        def xps(i, k, c):
            if k == "O":
                return bank[:, 6 + c, :]
            if k == "B":
                return place(i, "x", c)[0]
            return tps[:, c, :]

        def step_xb(i):
            return 2 if i.live() else 0

        def step_gate(i, k):
            return 3 if k == "B" and i.live() else 0

        def step_q(i):
            return len(units(i)) + (1 if (i - 3).live() else 2)

        st_a = qs[0][:, :, :].rearrange("p h s -> p (h s)").bitcast(fp32)
        st_c = qs[1][:, :, :].rearrange("p h s -> p (h s)").bitcast(fp32)
        SWO = C * 3 * D
        SG = SWO + C * D
        st_w1, st_w2 = st_a[:, 0:WKD], st_a[:, WKD:2 * WKD]
        st_qkv, st_wo, st_g = st_c[:, 0:SWO], st_c[:, SWO:SG], st_c[:, SG:SG + C * NEXP]
        BROW = (0, 32)
        st_b = [t_[r:r + 3, :, :].rearrange("p t n -> p (t n)") for r, t_ in zip(BROW, (acc["B"], xhat))]
        rowsum = sb("rowsum", [P, 2, NEXP * C])
        bsum = sb("bsum", [64, 2, NEXP])
        bpart = qkp[0].rearrange("p a c s -> p a (c s)")

        def drive(eng, iteration):
            first = 4
            loops = max(NSEQ - 1 - first, 0) // 2
            for i in range(min(first, NSEQ + 3)):
                iteration(Seq(i))
            if loops:
                with eng.Fori(0, loops) as r:
                    for o in range(2):
                        iteration(Seq(first + o, r))
            for i in range(first + 2 * loops, NSEQ + 3):
                iteration(Seq(i))

        NLOAD = 8 + 6 + 2 * C + 2
        NPOOL = 9 + NEXP - 1 + 5 + 4
        NDVE = 2 * (6 + 3 * 2 + 2) + 10
        MISC_PER = 4

        block = ctx.enter_context(nc.Block())

        @block.sync
        def _(eng):
            n = [0]

            def cld(dst, src):
                n[0] += 1
                eng.dma_start(dst, src, allow_slow_non_contiguous=True).then_inc(sem["weights_loaded"], 16)

            cld(acc["A"][:, :, :], x[0, :, :].rearrange("(t p) d -> p t d", p=P))
            cld(st_w1.rearrange("p (a n) -> p a n", n=D), W1.rearrange("e (c p) n -> p (e c) n", p=P))
            cld(st_w2.rearrange("p (a n) -> p a n", n=D), W2.rearrange("e (c p) n -> p (e c) n", p=P))
            cld(st_qkv.rearrange("p (c n) -> p c n", c=C)[:, :, 0:D], Wq.rearrange("(c p) n -> p c n", p=P))
            cld(st_qkv.rearrange("p (c n) -> p c n", c=C)[:, :, D:3 * D], Wkv.rearrange("(c p) n -> p c n", p=P))
            cld(st_wo.rearrange("p (c n) -> p c n", c=C), Wo.rearrange("(c p) n -> p c n", p=P))
            cld(st_g.rearrange("p (c n) -> p c n", c=C), gate_W.rearrange("(c p) n -> p c n", p=P))
            cld(gb[:, :], gate_b.rearrange("(n o) -> n o", o=1))
            for m, b in enumerate((b1, b2)):
                for r in range(3):
                    cld(st_b[m][r:r + 1, :], b.rearrange("(o e) n -> o (e n)", o=1))
            for c in range(C):
                cld(g1c[:, :, c], g1[:, c * P:(c + 1) * P].rearrange("e p -> p e"))
                cld(be1c[:, :, c], be1[:, c * P:(c + 1) * P].rearrange("e p -> p e"))
            for dst, src in ((g2b, g2), (be2b, be2)):
                cld(dst[:, :, :].rearrange("p e n -> p (e n)"),
                    src.rearrange("(o e) n -> o (e n)", o=1).broadcast_to([P, NEXP * D]))
            assert n[0] == NLOAD, (n, NLOAD)

            def rows(t, b):
                v = t[b.n, :, :] if b.reg is None else \
                    t[bass.ds(b.reg * 2 + b.n, 1), :, :].rearrange("o s d -> (o s) d")
                return v.rearrange("(t p) d -> p t d", p=P)

            def iteration(i):
                b = i
                if b.live():
                    eng.wait_ge(sem["z_summed_A"], at("z_summed_A", b))
                    settled(eng)
                    eng.dma_start(rows(out, b), acc["A"][:, :, :]).then_inc(sem["x1_kept"], 16)
                b = Seq(i.n + 1, i.reg)
                if b.live():
                    eng.wait_ge(sem["x1_kept"], at("x1_kept", i))
                    settled(eng)
                    eng.wait_ge(sem["ln_ready_Q"], at("ln_ready_Q", i))
                    settled(eng)
                    eng.dma_start(acc["A"][:, :, :], rows(x, b)).then_inc(sem["x_loaded"], 16)
                b = i - 3
                if b.live():
                    eng.wait_ge(sem["z_summed_B"], at("z_summed_B", b))
                    settled(eng)
                    eng.dma_start(rows(out, b), acc["B"][:, :, :]).then_inc(sem["out_stored"], 16)
                b = i - 2
                if b.live():
                    eng.wait_ge(sem["x1_kept"], at("x1_kept", b))
                    settled(eng)
                    eng.wait_ge(sem["attention_added"], at("attention_added", b - 1))
                    settled(eng)
                    eng.wait_ge(sem["pv_ready"], at("pv_ready", b))
                    settled(eng)
                    eng.dma_start(res[:, :, :], rows(out, b)).then_inc(sem["x1_back"], 16)
                b = i - 1
                if b.live():
                    eng.wait_ge(sem["maxima_copied"], at("maxima_copied", b))
                    settled(eng)
                    for p in range(3):
                        eng.dma_start(qs[b.s][KR + p:KR + p + 1, :, :], nmt[p * H:(p + 1) * H, :]).then_inc(sem["maxima_placed"], 16)
                b = i
                if b.live():
                    eng.wait_ge(sem["stacks_placed"], at("stacks_placed", b - 1))
                    settled(eng)
                    for n_ in range(2):
                        eng.wait_ge(sem["qk_part3"], at("qk_part3", b, C * (n_ + 1)))
                        settled(eng)
                        eng.dma_start(scratch[n_, :, :, :, :].rearrange("a c p s -> p a c s"),
                                      qkp[n_]).then_inc(sem["parts_stored"], 16)
                    eng.wait_ge(sem["keys_scored"], at("keys_scored", b - 2))
                    settled(eng)
                    for n_, (dst, part) in enumerate(((qs, QPART), (ks, KPART))):
                        eng.wait_ge(sem["parts_stored"], at("parts_stored", b))
                        settled(eng)
                        for g in range(G):
                            eng.dma_start(dst[b.s][g * HD:(g + 1) * HD, :, :],
                                          scratch[n_, part[g], :, :, :].rearrange("c (hc d) s -> d (c hc) s", d=HD)
                                          ).then_inc(sem["stacks_placed"], 16)

            drive(eng, iteration)
            eng.wait_ge(sem["out_stored"], at("out_stored", Seq(NSEQ - 1)))
            eng.wait_ge(sem["x_loaded"], at("x_loaded", Seq(NSEQ - 2)))
            eng.wait_ge(sem["stacks_placed"], at("stacks_placed", Seq(NSEQ - 1)))


        @block.gpsimd
        def _(eng):
            cp = [0]

            def step(ins):
                cp[0] += 1
                ins.then_inc(sem["pool_setup"], 1)
                eng.wait_ge(sem["pool_setup"], cp[0])

            step(eng.memset(identf[:, :], 0.0))
            step(eng.affine_select(out=identf[:, :], in_=identf[:, :], compare_op=ALU.not_equal, fill=1.0,
                                   base=0, pattern=[[-1, P]], channel_multiplier=1))
            step(eng.tensor_copy(identb[:, :], identf[:, :]))
            step(eng.memset(mask_q[:, :], 0.0))
            step(eng.affine_select(out=mask_q[:, :], in_=mask_q[:, :], compare_op=ALU.is_ge, fill=MASKED,
                                   base=0, pattern=[[-1, P]], channel_multiplier=1))
            step(eng.memset(mask_k[:, :], 0.0))
            step(eng.affine_select(out=mask_k[:, :], in_=mask_k[:, :], compare_op=ALU.is_ge, fill=MASKED,
                                   base=0, pattern=[[1, P]], channel_multiplier=-1))
            step(eng.memset(neghalf[:, :], -0.5))
            step(eng.memset(lower[:, :, :, :], 0.0))
            for e in range(NEXP):
                if e:
                    step(eng.memset(lower[:, :, e, 0:e], 1.0))
            for m, r in enumerate(BROW):
                step(eng.memset(ones3[m][:, :], 0.0))
                step(eng.memset(ones3[m][r:r + 3, :], 1.0))
            step(eng.memset(bias[:, :, :], 0.0))
            for s in range(2):
                step(eng.memset(ks[s][64:P, :, :], 1.0))
                step(eng.memset(va[s][:, :, :, HD:HD + 1], 1.0))
            assert cp[0] == NPOOL, (cp, NPOOL)

            def ln(k, b):
                eng.wait_ge(sem[f"ln_stats_{k}"], at(f"ln_stats_{k}", b))
                settled(eng)
                eng.tensor_scalar(rtmp[k][:, :], mv[k][:, :, 1], LN_EPS, None, ALU.add).then_inc(sem[f"ln_var_{k}"], 1)
                eng.wait_ge(sem[f"ln_var_{k}"], at(f"ln_var_{k}", b))
                eng.tensor_tensor(rstd[k][:, :], rtmp[k][:, :], neghalf[:, 0:T], ALU.pow).then_inc(sem[f"ln_rstd_{k}"], 1)

            def iteration(i):
                us = units(i)
                b_ = i - 3
                for s in range(len(us) + 3):
                    if b_.live() and s == (1 if i.live() else 0):
                        ln("B", b_)
                    if i.live() and b_.live() and s == step_q(i) - 2:
                        ln("Q", i)
                    if s < len(us):
                        k, b, e = us[s]
                        eng.wait_ge(sem[f"y_squares_{k}"], at(f"y_squares_{k}", b, e + 1))
                        eng.wait_ge(sem[f"y_normed_{k}"], at(f"y_normed_{k}", b, 2 * e))
                        settled(eng)
                        eng.tensor_scalar(tmp1[k][:, :], ss1[k][:, :], 1.0 / D, LN_EPS, ALU.mult,
                                          ALU.add).then_inc(sem[f"y_var_{k}"], 1)
                        eng.wait_ge(sem[f"y_var_{k}"], at(f"y_var_{k}", b, e + 1))
                        eng.tensor_tensor(rs1[k][:, :], tmp1[k][:, :], neghalf[:, 0:T],
                                          ALU.pow).then_inc(sem[f"y_rstd_{k}"], 1)
                    if s >= 3:
                        k, b, e = us[s - 3]
                        eng.wait_ge(sem[f"z_shifted_{k}"], at(f"z_shifted_{k}", b, e + 1))
                        eng.wait_ge(sem[f"z_scaled_{k}"], at(f"z_scaled_{k}", b, 2 * e + 2))
                        eng.tensor_tensor(acc[k][:, :, :], acc[k][:, :, :], u[:, :, :], ALU.add).then_inc(sem[f"z_summed_{k}"], 1)
                    if 2 <= s < len(us) + 2:
                        k, b, e = us[s - 2]
                        eng.wait_ge(sem[f"z_squares_{k}"], at(f"z_squares_{k}", b, e + 1))
                        if e == 0:
                            eng.wait_ge(sem[f"gate_step_{k}"], at(f"gate_step_{k}", b))
                        settled(eng)
                        eng.tensor_scalar(tmp2[k][:, :], ss2[k][:, :], 1.0 / D, LN_EPS, ALU.mult,
                                          ALU.add).then_inc(sem[f"z_var_{k}"], 1)
                        eng.wait_ge(sem[f"z_var_{k}"], at(f"z_var_{k}", b, e + 1))
                        eng.tensor_tensor(rs2[k][:, :], tmp2[k][:, :], neghalf[:, 0:T],
                                          ALU.pow).then_inc(sem[f"z_rstd_{k}"], 1)
                        eng.wait_ge(sem[f"z_rstd_{k}"], at(f"z_rstd_{k}", b, e + 1))
                        eng.wait_ge(sem[f"z_scaled_{k}"], at(f"z_scaled_{k}", b, 2 * e))
                        eng.tensor_tensor(wst[k][:, :], rs2[k][:, :], wgt[k][:, :, e], ALU.mult).then_inc(sem[f"z_factor_{k}"], 1)
                if i.live() and not b_.live():
                    ln("Q", i)
                if Seq(i.n + 1, i.reg).live():
                    ln("A", Seq(i.n + 1, i.reg))
                if i.live():
                    for n_ in range(2 * C):
                        eng.wait_ge(sem["qk_part2"], at("qk_part2", i, n_ + 1))
                        eng.tensor_tensor(qkp[n_ // C][:, 2, n_ % C, :], qkr[:, n_ % 2, :],
                                              qkp[n_ // C][:, 1, n_ % C, :], ALU.subtract).then_inc(sem["qk_part3"], 1)

            ln("A", Seq(0))
            drive(eng, iteration)


        @block.scalar
        def _(eng):
            def high(i, k, b):
                for c in range(C):
                    eng.wait_ge(sem[f"x_turned_{k}"], at(f"x_turned_{k}", b, c + 1))
                    eng.activation(xt[k][0][:, c, :], xps(i, k, c), ACT.Copy).then_inc(sem[f"x_high_{k}"], 1)

            def squares(i, us, s):
                if s >= 2:
                    k, b, e = us[s - 2]
                    eng.wait_ge(sem[f"z_var_{k}"], at(f"z_var_{k}", b, e))
                    if s < len(us):
                        eng.wait_ge(sem[f"y_squares_{us[s][0]}"], at(f"y_squares_{us[s][0]}", us[s][1], us[s][2] + 1))
                    else:
                        kk, bb, ee = us[s - 3] if s > 2 else us[-1]
                        eng.wait_ge(sem[f"z_squares_{kk}" if s > 2 else f"y_squares_{kk}"], at(f"z_squares_{kk}" if s > 2 else f"y_squares_{kk}", bb, ee + 1))
                        eng.wait_ge(sem[f"y_squares_{us[-1][0]}"], at(f"y_squares_{us[-1][0]}", us[-1][1]))
                    for t in range(T):
                        if t % 2 == 0:
                            eng.wait_ge(sem[f"z_ready_{k}"], at(f"z_ready_{k}", b, 2 * e + t // 2 + 1))
                        ins = eng.activation(junk[:, t, :], place(i, "z", s - 2, t // 2)[0][:, (t % 2) * D:(t % 2 + 1) * D],
                                             ACT.Square, accum_out=ss2[k][:, t:t + 1])
                    ins.then_inc(sem[f"z_squares_{k}"], 1)

            def high_h(i, us, s):
                if 1 <= s <= len(us):
                    k, b, e = us[s - 1]
                    if s >= 2:
                        kk, bb, ee = us[s - 2]
                        eng.wait_ge(sem[f"z_ready_{kk}"], at(f"z_ready_{kk}", bb, 2 * ee + 2))
                    for c in range(C):
                        eng.activation(hh[:, c, :], tps[:, c, :], ACT.Relu,
                                       bias=be1c[:, e, c:c + 1], scale=g1c[:, e, c:c + 1]).then_inc(sem[f"h_high_{k}"], 1)

            def iteration(i):
                us = units(i)
                b_ = i - 3
                for s in range(len(us) + 2):
                    if b_.live() and not i.live() and s == 0:
                        high(i, "B", b_)
                    if i.live() and b_.live() and s == step_q(i):
                        high(i, "Q", i)
                    if s < len(us):
                        k, b, e = us[s]
                        eng.wait_ge(sem[f"y_var_{k}"], at(f"y_var_{k}", b, e))
                        if s:
                            kk, bb, ee = us[s - 1]
                            eng.wait_ge(sem[f"y_squares_{kk}"], at(f"y_squares_{kk}", bb, ee + 1))
                            if s > 2:
                                kk, bb, ee = us[s - 3]
                                eng.wait_ge(sem[f"z_squares_{kk}"], at(f"z_squares_{kk}", bb, ee + 1))
                        else:
                            for kk, bb in (("A", i - 1), ("B", i - 4)):
                                if bb.live():
                                    eng.wait_ge(sem[f"z_squares_{kk}"], at(f"z_squares_{kk}", bb))
                        for t in range(T):
                            if t % 2 == 0:
                                eng.wait_ge(sem[f"y_ready_{k}"], at(f"y_ready_{k}", b, 2 * e + t // 2 + 1))
                            ins = eng.activation(junk[:, t, :], yhalf(s, t // 2)[:, (t % 2) * D:(t % 2 + 1) * D],
                                                 ACT.Square, accum_out=ss1[k][:, t:t + 1])
                        ins.then_inc(sem[f"y_squares_{k}"], 1)
                    if 1 <= s <= len(us):
                        k, b, e = us[s - 1]
                        if s == 1 and (i - 1).live():
                            eng.wait_ge(sem["qk_part3"], at("qk_part3", i - 1))
                        if s >= 2:
                            kk, bb, ee = us[s - 2]
                            eng.wait_ge(sem[f"h_low_{kk}"], at(f"h_low_{kk}", bb, 2 * ee + 2))
                        for c in range(C):
                            eng.wait_ge(sem[f"y_turned_{k}"], at(f"y_turned_{k}", b, 2 * e + c + 1))
                            eng.activation(hf[:, c, :], tps[:, c, :], ACT.Relu,
                                               bias=be1c[:, e, c:c + 1], scale=g1c[:, e, c:c + 1]).then_inc(sem[f"h_ready_{k}"], 1)
                    if b_.live() and i.live() and s == step_xb(i):
                        high(i, "B", b_)
                    if s == len(us):
                        high_h(i, us, s)
                        squares(i, us, s)
                    else:
                        squares(i, us, s)
                        high_h(i, us, s)
                    for k, b in (("A", i), ("B", b_)):
                        if b.live() and s == max(1, step_gate(i, k)):
                            eng.wait_ge(sem[f"gate_step_{k}"], at(f"gate_step_{k}", b, 2))
                            eng.activation(gexp[k][:, :, :], gcmp[:, :, 0, :], ACT.Exp).then_inc(sem[f"gate_exp_{k}"], 1)
                if i.live() and not b_.live():
                    high(i, "Q", i)
                m, e_ = i - 1, i - 2
                if e_.live():
                    for h in range(H):
                        if h == 0:
                            for k, b in (("A", i), ("B", i - 3)):
                                if b.live():
                                    eng.wait_ge(sem[f"z_summed_{k}"], at(f"z_summed_{k}", b))
                            eng.wait_ge(sem["parts_stored"], at("parts_stored", i - 1))
                        if h >= NPT:
                            eng.wait_ge(sem["pv_ready"], at("pv_ready", e_, (h - NPT) // QUAD + 1))
                        for p in range(2):
                            eng.wait_ge(sem["keys_scored"], at("keys_scored", e_, 2 * h + p + 1))
                            eng.activation(pt[:, h % NPT, PCOL[p]:PCOL[p + 1]], eps_[:, PCOL[p]:PCOL[p + 1]], ACT.Exp,
                                           scale=SCALE).then_inc(sem["exp_ready"], 1)
                        if h % QUAD == 1 and h >= QUAD:
                            o_copy(e_, h // QUAD - 1)
                    o_copy(e_, QUAD - 1)
                nxt = Seq(i.n + 1, i.reg)

                def parts(n0):
                    for n_ in (n0, n0 + 1):
                        eng.wait_ge(sem["qk_ready"], at("qk_ready", i, n_ + 1))
                        if n_ == 0:
                            eng.wait_ge(sem["parts_stored"], at("parts_stored", i - 1))
                        eng.activation(qkp[n_ // C][:, 0, n_ % C, :], qkb[n_], ACT.Copy).then_inc(sem["qk_part1"], 1)

                def second(n0):
                    for n_ in (n0, n0 + 1):
                        eng.wait_ge(sem["qk_rest"], at("qk_rest", i, n_ + 1))
                        eng.activation(qkp[n_ // C][:, 1, n_ % C, :], qkr[:, n_ % 2, :], ACT.Copy).then_inc(sem["qk_part2"], 1)

                if i.live():
                    parts(0)
                    second(0)
                if m.live():
                    eng.wait_ge(sem["maxima_turned"], at("maxima_turned", m))
                    eng.wait_ge(sem["maxima_placed"], at("maxima_placed", m - 1))
                    eng.activation(nmt[:, :], rps.bitcast(bf16)[0:3 * H, 0:S], ACT.Copy).then_inc(sem["maxima_copied"], 1)
                if nxt.live():
                    high(i, "A", nxt)
                if i.live():
                    parts(2)
                if e_.live():
                    high(i, "O", e_)
                if i.live():
                    second(2)

            def o_copy(b, g):
                eng.wait_ge(sem["pv_ready"], at("pv_ready", b, g + 1))
                eng.wait_ge(sem["pv_turned"], at("pv_turned", b, g))
                eng.activation(ot[:, :], ops, ACT.Copy).then_inc(sem["pv_copied"], 1)

            high(Seq(0), "A", Seq(0))
            drive(eng, iteration)

        @block.vector
        def _(eng):
            eng.wait_ge(sem["weights_loaded"], 16 * NLOAD)
            eng.wait_ge(sem["pool_setup"], NPOOL)
            cd = [0]

            def step(ins):
                cd[0] += 1
                ins.then_inc(sem["dve_setup"], 1)
                eng.wait_ge(sem["dve_setup"], cd[0])

            for m, (st, w) in enumerate(((st_w1, w1), (st_w2, w2))):
                v = st.rearrange("p (a n) -> p a n", n=D)
                step(eng.tensor_reduce(rowsum[:, m, :], v, AX.X, ALU.add))
                step(eng.tensor_scalar(rowsum[:, m, :], rowsum[:, m, :], -1.0 / D, None, ALU.mult))
                step(eng.tensor_tensor(v, v, rowsum[:, m, :].unsqueeze(2).broadcast_to([P, NEXP * C, D]), ALU.add))
                b = st_b[m].rearrange("p (a n) -> p a n", n=D)
                bs = bsum[BROW[m]:BROW[m] + 3, m, :]
                step(eng.tensor_reduce(bs, b, AX.X, ALU.add))
                step(eng.tensor_scalar(bs, bs, -1.0 / D, None, ALU.mult))
                step(eng.tensor_tensor(b, b, bs.unsqueeze(2).broadcast_to([3, NEXP, D]), ALU.add))
                r0 = BROW[m]
                dst = bias[r0:r0 + 3, :, :].rearrange("p e n -> p (e n)")
                bp = bpart[r0:r0 + 3, :, :]
                for r in range(3):
                    step(eng.tensor_copy(bp[:, r, :], st_b[m]))
                    if r < 2:
                        step(eng.tensor_tensor(st_b[m], st_b[m], bp[:, r, :], ALU.subtract))
                    if r == 0:
                        step(eng.tensor_scalar(dst, bp[:, 0, :], identf[r0:r0 + 3, r0:r0 + 1], None, ALU.mult))
                    else:
                        step(eng.scalar_tensor_tensor(out=dst, in0=bp[:, r, :], scalar=identf[r0:r0 + 3, r0 + r:r0 + r + 1], in1=dst,
                                                      op0=ALU.mult, op1=ALU.add))
            for st, w in ((st_w1, w1), (st_w2, w2), (st_qkv, wqkv), (st_wo, wo), (st_g, gw)):
                flat = [w_[:, :, :, :].rearrange("p e c n -> p (e c n)") if len(w_.shape) == 4 else
                        w_[:, :, :].rearrange("p c n -> p (c n)") for w_ in w]
                step(eng.tensor_copy(flat[0], st))
                step(eng.tensor_tensor(flat[1], st, flat[0].bitcast(fp32), ALU.subtract))
            assert cd[0] == NDVE, (cd, NDVE)

            def ln(k, b, src):
                for t in range(T):
                    ins = eng.bn_stats(out=st6[k][:, t, :], in_=src[:, t, :])
                ins.then_inc(sem[f"ln_parts_{k}"], 1)
                eng.wait_ge(sem[f"ln_parts_{k}"], at(f"ln_parts_{k}", b))
                settled(eng)
                for t in range(T):
                    ins = eng.bn_aggr(out=mv[k][:, t, :], in_=st6[k][:, t, :])
                ins.then_inc(sem[f"ln_stats_{k}"], 1)

            def ln_out(k, b, src):
                eng.wait_ge(sem[f"ln_rstd_{k}"], at(f"ln_rstd_{k}", b))
                for t in range(T):
                    ins = eng.tensor_scalar(xhat[:, t, :], src[:, t, :], mv[k][:, t, 0:1], rstd[k][:, t:t + 1],
                                            ALU.subtract, ALU.mult)
                ins.then_inc(sem[f"ln_ready_{k}"], 1)

            def begin(k, b):
                eng.wait_ge(sem[f"ln_ready_{k}"], at(f"ln_ready_{k}", b))
                eng.scalar_tensor_tensor(out=acc[k][:, :, :], in0=xhat[:, :, :], scalar=0.5, in1=acc[k][:, :, :],
                                         op0=ALU.mult, op1=ALU.add).then_inc(sem[f"sum_begun_{k}"], 1)

            def biased(i, k, b):
                eng.wait_ge(sem[f"gate_ready_{k}"], at(f"gate_ready_{k}", b))
                eng.tensor_scalar(gt, place(i, "gate", k)[0][0:NEXP, :], gb[:, 0:1], None,
                                  ALU.add).then_inc(sem[f"gate_biased_{k}"], 1)

            def add_attention(i, b):
                eng.wait_ge(sem["x1_back"], at("x1_back", b))
                eng.wait_ge(sem["out_stored"], at("out_stored", b - 1))
                for j in range(2):
                    eng.wait_ge(sem["wo_ready"], at("wo_ready", b, j + 1))
                    ins = eng.tensor_tensor(acc["B"][:, 2 * j:2 * j + 2, :],
                                            place(i, "wo", j)[0].rearrange("p (t n) -> p t n", t=2),
                                            res[:, 2 * j:2 * j + 2, :], ALU.add)
                ins.then_inc(sem["attention_added"], 1)
                eng.wait_ge(sem["attention_added"], at("attention_added", b))
                ln("B", b, acc["B"])

            def low(i, k, b):
                for c in range(C):
                    eng.wait_ge(sem[f"x_high_{k}"], at(f"x_high_{k}", b, c + 1))
                    eng.tensor_tensor(xt[k][1][:, c, :], xps(i, k, c), xt[k][0][:, c, :].bitcast(fp32),
                                          ALU.subtract).then_inc(sem[f"x_low_{k}"], 1)

            def gate(i, k, b):
                n = [0]

                def g(ins, w=True):
                    ins.then_inc(sem[f"gate_step_{k}"], 1)
                    n[0] += 1
                    if w:
                        eng.wait_ge(sem[f"gate_step_{k}"], at(f"gate_step_{k}", b, n[0]))

                eng.wait_ge(sem[f"gate_turned_{k}"], at(f"gate_turned_{k}", b))
                g(eng.tensor_copy(gs[k][:, :, :], place(i, "gate", k)[0][:, 0:T * NEXP].rearrange("p (t e) -> p t e", e=NEXP)))
                eng.tensor_reduce(gmax[k][:, :], gs[k][:, :, :], AX.X, ALU.max).then_inc(sem["gate_reduced"], 1)
                waitmisc(b)
                g(eng.tensor_tensor(gcmp[:, :, 0, :], gs[k][:, :, :],
                                    gmax[k][:, :].unsqueeze(2).broadcast_to([P, T, NEXP]), ALU.subtract), False)
                mine = gs[k][:, :, :].unsqueeze(3).broadcast_to([P, T, NEXP, NEXP])
                other = gs[k][:, :, :].unsqueeze(2).broadcast_to([P, T, NEXP, NEXP])
                eng.wait_ge(sem[f"gate_exp_{k}"], at(f"gate_exp_{k}", b))
                g(eng.tensor_tensor(gcmp[:, :, :, :], other, mine, ALU.is_gt))
                g(eng.tensor_tensor(gcmq[:, :, :, :], other, mine, ALU.is_equal))
                g(eng.tensor_tensor(gcmq[:, :, :, :], gcmq[:, :, :, :], lower[:, :, :, :], ALU.mult))
                g(eng.tensor_tensor(gcmp[:, :, :, :], gcmp[:, :, :, :], gcmq[:, :, :, :], ALU.add))
                g(eng.tensor_reduce(grank[k][:, :, :], gcmp[:, :, :, :], AX.X, ALU.add))
                g(eng.scalar_tensor_tensor(out=gexp[k][:, :, :], in0=grank[k][:, :, :], scalar=1.5,
                                           in1=gexp[k][:, :, :], op0=ALU.is_lt, op1=ALU.mult))
                eng.tensor_reduce(gsum[k][:, :], gexp[k][:, :, :], AX.X, ALU.add).then_inc(sem["gate_reduced"], 1)
                waitmisc(b)
                g(eng.reciprocal(gsum[k][:, :], gsum[k][:, :]))
                g(eng.scalar_tensor_tensor(out=wgt[k][:, :, :], in0=gexp[k][:, :, :], scalar=0.5,
                                           in1=gsum[k][:, :].unsqueeze(2).broadcast_to([P, T, NEXP]),
                                           op0=ALU.mult, op1=ALU.mult))
                assert n[0] == per[f"gate_step_{k}"]

            misc = {"n": 0, "reg": None, "per": 0}

            def waitmisc(b):
                misc["n"] += 1
                v = misc["n"]
                if misc["reg"] is None:
                    eng.wait_ge(sem["gate_reduced"], v)
                else:
                    eng.wait_ge(sem["gate_reduced"], misc["reg"] * misc["per"] + v)

            def iteration(i):
                if i.reg is None and misc["reg"] is not None:
                    misc["n"] += misc["per"] * (misc["loops"] - 1)
                    misc["reg"] = None
                if i.reg is not None:
                    misc["reg"], misc["per"], misc["loops"] = i.reg, 2 * MISC_PER, (NSEQ - 5) // 2
                us = units(i)
                b_ = i - 3
                nxt = Seq(i.n + 1, i.reg)
                m, e_ = i - 1, i - 2
                early = b_.live() or not i.live()
                for s in range(len(us) + 2):
                    if b_.live() and not i.live() and s == 0:
                        add_attention(i, b_)
                        ln_out("B", b_, acc["B"])
                        begin("B", b_)
                        low(i, "B", b_)
                    for k, b in (("A", i), ("B", b_)):
                        if b.live() and s == step_gate(i, k):
                            biased(i, k, b)
                    if s < len(us):
                        k, b, e = us[s]
                        eng.wait_ge(sem[f"y_rstd_{k}"], at(f"y_rstd_{k}", b, e + 1))
                        if s:
                            kk, bb, ee = us[s - 1]
                            eng.wait_ge(sem[f"y_turned_{kk}"], at(f"y_turned_{kk}", bb, 2 * ee + 2))
                        for j in range(2):
                            y = yhalf(s, j).rearrange("p (t n) -> p t n", t=2)
                            eng.tensor_tensor(yn[:, 2 * j:2 * j + 2, :], y,
                                                  rs1[k][:, 2 * j:2 * j + 2].unsqueeze(2).broadcast_to([P, 2, D]),
                                                  ALU.mult).then_inc(sem[f"y_normed_{k}"], 1)
                    if b_.live() and i.live() and s == 0:
                        add_attention(i, b_)
                    if b_.live() and i.live() and s == 1:
                        eng.wait_ge(sem["x_turned_A"], at("x_turned_A", i))
                        ln_out("B", b_, acc["B"])
                        begin("B", b_)
                    if b_.live() and i.live() and s == step_xb(i):
                        low(i, "B", b_)
                    if 1 <= s <= len(us):
                        k, b, e = us[s - 1]
                        if s >= 2:
                            kk, bb, ee = us[s - 2]
                            eng.wait_ge(sem[f"z_ready_{kk}"], at(f"z_ready_{kk}", bb, 2 * ee + 2))
                        for c in range(C):
                            eng.wait_ge(sem[f"h_ready_{k}"], at(f"h_ready_{k}", b, 2 * e + c + 1))
                            eng.wait_ge(sem[f"h_high_{k}"], at(f"h_high_{k}", b, 2 * e + c + 1))
                            eng.tensor_tensor(hl[:, c, :], hf[:, c, :], hh[:, c, :].bitcast(fp32),
                                              ALU.subtract).then_inc(sem[f"h_low_{k}"], 1)
                    if i.live() and b_.live() and s == step_q(i):
                        low(i, "Q", i)
                    if m.live() and early and s >= len(us):
                        reduce(m, s - len(us))
                    if i.live() and b_.live() and s == step_q(i) - 3:
                        eng.wait_ge(sem["z_summed_A"], at("z_summed_A", i))
                        ln("Q", i, acc["A"])
                    if s >= 2:
                        k, b, e = us[s - 2]
                        eng.wait_ge(sem[f"z_factor_{k}"], at(f"z_factor_{k}", b, e + 1))
                        if s >= 3:
                            kk, bb, ee = us[s - 3]
                            eng.wait_ge(sem[f"z_summed_{kk}"], at(f"z_summed_{kk}", bb, ee + 1))
                        for t in range(T):
                            ins = eng.scalar_tensor_tensor(
                                out=u[:, t, :], in0=place(i, "z", s - 2, t // 2)[0][:, (t % 2) * D:(t % 2 + 1) * D],
                                scalar=wst[k][:, t:t + 1], in1=g2b[:, e, :], op0=ALU.mult, op1=ALU.mult)
                            if t % 2:
                                ins.then_inc(sem[f"z_scaled_{k}"], 1)
                        if e == 0:
                            eng.wait_ge(sem[f"sum_begun_{k}"], at(f"sum_begun_{k}", b))
                        else:
                            eng.wait_ge(sem[f"z_summed_{k}"], at(f"z_summed_{k}", b, e))
                        for t in range(T):
                            ins = eng.scalar_tensor_tensor(
                                out=acc[k][:, t, :], in0=be2b[:, e, :], scalar=wgt[k][:, t, e:e + 1], in1=acc[k][:, t, :],
                                op0=ALU.mult, op1=ALU.add)
                        ins.then_inc(sem[f"z_shifted_{k}"], 1)
                    if i.live() and b_.live() and s == step_q(i) - 2:
                        eng.wait_ge(sem["x_turned_B"], at("x_turned_B", b_))
                        ln_out("Q", i, acc["A"])
                    for k, b in (("A", i), ("B", b_)):
                        if b.live() and s == max(1, step_gate(i, k)):
                            gate(i, k, b)
                if i.live() and not b_.live():
                    eng.wait_ge(sem["z_summed_A"], at("z_summed_A", i))
                    ln("Q", i, acc["A"])
                    ln_out("Q", i, acc["A"])
                    low(i, "Q", i)
                for h in range(H):
                    if m.live():
                        for g in range(2 if early else 0, LEAD + 1) if h == 0 else range(h + LEAD, min(h + LEAD + 1, H)):
                            reduce(m, g)
                    if e_.live() and h % QUAD == QUAD - 1 and h >= QUAD:
                        normalise(e_, h // QUAD - 1)
                    if nxt.live() and h == 4:
                        eng.wait_ge(sem["x_loaded"], at("x_loaded", i))
                        ln("A", nxt, acc["A"])
                    if nxt.live() and h == 6:
                        eng.wait_ge(sem["x_turned_Q"], at("x_turned_Q", i))
                        ln_out("A", nxt, acc["A"])
                    if nxt.live() and h == 8:
                        begin("A", nxt)
                if m.live():
                    eng.wait_ge(sem["block_maxima"], at("block_maxima", m))
                    for t in range(T):
                        o = MCOL[t] // P
                        ins = eng.tensor_reduce(nm[:, t, :], bm[:, :, o:o + t + 1], AX.X, ALU.max, negate=True)
                    ins.then_inc(sem["maxima_ready"], 1)
                    eng.wait_ge(sem["maxima_ready"], at("maxima_ready", m))
                    eng.wait_ge(sem["maxima_turned"], at("maxima_turned", m - 1))
                    src = nm
                    for p in range(3):
                        eng.tensor_copy(nmp[:, :, p, :], src[:, :, :]).then_inc(sem["maxima_part"], 1)
                        if p < 2:
                            eng.wait_ge(sem["maxima_part"], at("maxima_part", m, p + 1))
                            eng.tensor_tensor(nmr[:, :, :], src[:, :, :], nmp[:, :, p, :], ALU.subtract).then_inc(sem["maxima_rest"], 1)
                            eng.wait_ge(sem["maxima_rest"], at("maxima_rest", m, p + 1))
                        src = nmr

                def rest(n_):
                    eng.wait_ge(sem["qk_part1"], at("qk_part1", i, n_ + 1))
                    if n_ >= 2:
                        eng.wait_ge(sem["qk_part3"], at("qk_part3", i, n_ - 1))
                    eng.tensor_tensor(qkr[:, n_ % 2, :], qkb[n_], qkp[n_ // C][:, 0, n_ % C, :],
                                      ALU.subtract).then_inc(sem["qk_rest"], 1)

                if i.live():
                    for j in range(2):
                        eng.wait_ge(sem["v_ready"], at("v_ready", i, j + 1))
                        eng.tensor_copy(va[i.s][:, 2 * j:2 * j + 2, :, 0:HD],
                                            bank[:, 3 + j, :].rearrange("p (t h d) -> p t h d", t=2, h=H)).then_inc(sem["v_copied"], 1)
                if e_.live():
                    normalise(e_, QUAD - 1)
                if i.live():
                    rest(0)
                    rest(1)
                if nxt.live():
                    low(i, "A", nxt)
                if i.live():
                    rest(2)
                    rest(3)
                if e_.live():
                    low(i, "O", e_)

            def reduce(m, h):
                for p in range(2):
                    eng.wait_ge(sem["queries_scored"], at("queries_scored", m, 2 * h + p + 1))
                    eng.tensor_reduce(bm[:, h, PCOL[p] // P:PCOL[p + 1] // P],
                                      mps[:, PCOL[p]:PCOL[p + 1]].rearrange("p (b n) -> p b n", n=P),
                                      AX.X, ALU.max).then_inc(sem["block_maxima"], 1)

            def normalise(b, g):
                if g == 0:
                    eng.wait_ge(sem["x_turned_O"], at("x_turned_O", b - 1))
                eng.wait_ge(sem["pv_turned"], at("pv_turned", b, g + 1))
                v = rps.rearrange("p (t q d) -> p t q d", t=T, q=QUAD)
                eng.reciprocal(rden[:, :, :], v[:, :, :, HD]).then_inc(sem["sums_inverted"], 1)
                eng.wait_ge(sem["sums_inverted"], at("sums_inverted", b, g + 1))
                eng.tensor_tensor(on[:, :, g * QUAD * HD:(g + 1) * QUAD * HD].rearrange("p t (q d) -> p t q d", q=QUAD),
                                      v[:, :, :, 0:HD], rden[:, :, :].unsqueeze(3).broadcast_to([P, T, QUAD, HD]),
                                      ALU.mult).then_inc(sem["pv_normed"], 1)

            ln("A", Seq(0), acc["A"])
            ln_out("A", Seq(0), acc["A"])
            begin("A", Seq(0))
            low(Seq(0), "A", Seq(0))
            drive(eng, iteration)


        @block.tensor
        def _(eng):
            eng.wait_ge(sem["pool_setup"], NPOOL)
            eng.wait_ge(sem["dve_setup"], NDVE)
            PROD = ((0, 0), (0, 1), (1, 0))

            def xpose(i, k, b):
                eng.wait_ge(sem[f"ln_ready_{k}"], at(f"ln_ready_{k}", b))
                for c in range(C):
                    for t in range(T):
                        mm = eng.transpose(xps(i, k, c)[:, t * P:(t + 1) * P], xhat[:, t, c * P:(c + 1) * P], identf[:, :])
                    mm.then_inc(sem[f"x_turned_{k}"], 1)

            def tokens(out_, lhs, rhs, m=None, e=None):
                n = 0
                for c in range(C):
                    for a, w in PROD:
                        n += 1
                        mm = eng.matmul(out_, lhs(a, c), rhs(w, c), start=(n == 1),
                                        stop=(n == 3 * C and m is None))
                if m is not None:
                    mm = eng.matmul(out_, ones3[m][:, :], bias[:, e, :], start=False, stop=True)
                return mm

            def gate_scores(i, k, b):
                out_, freed = place(i, "gate", k)
                if freed:
                    eng.wait_ge(sem[freed[0]], at(*freed))
                n = 0
                for c in range(C):
                    for a, w in PROD:
                        n += 1
                        mm = eng.matmul(out_[0:NEXP, :], gw[w][:, c, :], xt[k][a][:, c, :], start=(n == 1),
                                        stop=(n == 3 * C))
                mm.then_inc(sem[f"gate_ready_{k}"], 1)

            def gate_turn(i, k, b):
                out_ = place(i, "gate", k)[0]
                eng.wait_ge(sem[f"gate_biased_{k}"], at(f"gate_biased_{k}", b))
                settled(eng)
                for t in range(T):
                    mm = eng.transpose(out_[:, t * NEXP:(t + 1) * NEXP], gt[:, t * P:(t + 1) * P],
                                       identf[0:NEXP, 0:NEXP])
                mm.then_inc(sem[f"gate_turned_{k}"], 1)

            def project(i, b):
                for t in range(T):
                    out_, freed = place(i, "wo", t // 2)
                    if freed and t % 2 == 0:
                        eng.wait_ge(sem[freed[0]], at(*freed))
                    mm = tokens(out_[:, (t % 2) * D:(t % 2 + 1) * D],
                                lambda a, c: xt["O"][a][:, c, t * P:(t + 1) * P], lambda w, c: wo[w][:, c, :])
                    if t % 2:
                        mm.then_inc(sem["wo_ready"], 1)

            def turn_b(i, b):
                for c in range(C):
                    freed = place(i, "x", c)[1]
                    if freed:
                        eng.wait_ge(sem[freed[0]], at(*freed))
                xpose(i, "B", b)

            def zstep(i, us, s, tiles):
                k, b, e = us[s]
                eng.wait_ge(sem[f"h_low_{k}"], at(f"h_low_{k}", b, 2 * e + 2))
                hp = (hh, hl)
                for t in tiles:
                    out_, freed = place(i, "z", s, t // 2)
                    if freed and t % 2 == 0:
                        eng.wait_ge(sem[freed[0]], at(*freed))
                    mm = tokens(out_[:, (t % 2) * D:(t % 2 + 1) * D],
                                lambda a, c: hp[a][:, c, t * P:(t + 1) * P],
                                lambda w, c: w2[w][:, e, c, :], 1, e)
                    if t % 2:
                        mm.then_inc(sem[f"z_ready_{k}"], 1)

            def maxima(m, h):
                for p in range(2):
                    if h:
                        eng.wait_ge(sem["block_maxima"], at("block_maxima", m, 2 * h - 1 + p))
                    for t in MPART[p]:
                        o = MCOL[t]
                        w_ = (t + 1) * P
                        eng.matmul(mps[:, o:o + w_], qs[m.s][0:KR, h, t * P:(t + 1) * P], ks[m.s][0:KR, h, 0:w_],
                                   start=True, stop=False)
                        mm = eng.matmul(mps[:, o + w_ - P:o + w_], identb[:, :], mask_q[:, :], start=False,
                                        stop=True)
                    mm.then_inc(sem["queries_scored"], 1)

            def iteration(i):
                us = units(i)
                b_ = i - 3
                m, e_ = i - 1, i - 2

                def chunk(n_):
                    n = 0
                    for c in range(C):
                        for a, w in PROD:
                            n += 1
                            mm = eng.matmul(qkb[n_], wqkv[w][:, c, n_ * P:(n_ + 1) * P],
                                            xt["Q"][a][:, c, :], start=(n == 1), stop=(n == 3 * C))
                    mm.then_inc(sem["qk_ready"], 1)

                early = b_.live() or not i.live()
                if i.live():
                    eng.wait_ge(sem["x_low_A"], at("x_low_A", i))
                for s in range(len(us) + 2):
                    if b_.live() and not i.live() and s == 0:
                        if (i - 1).live():
                            eng.wait_ge(sem["qk_rest"], at("qk_rest", i - 1))
                        project(i, b_)
                        turn_b(i, b_)
                        eng.wait_ge(sem["x_low_B"], at("x_low_B", b_))
                        gate_scores(i, "B", b_)
                    if s == len(us):
                        zstep(i, us, s - 2, (0, 1))
                    if i.live() and b_.live() and s == step_q(i):
                        k, b, e = us[-1]
                        eng.wait_ge(sem[f"h_high_{k}"], at(f"h_high_{k}", b))
                        xpose(i, "Q", i)
                    if s < len(us):
                        k, b, e = us[s]
                        if e == 0 and k == "B":
                            eng.wait_ge(sem["x_low_B"], at("x_low_B", b))
                        for t in range(T):
                            if t % 2 == 0 and 2 * s + t // 2 >= 3:
                                kk, bb, ee = us[(2 * s + t // 2 - 3) // 2]
                                v = 2 * ee + (2 * s + t // 2 - 3) % 2 + 1
                                eng.wait_ge(sem[f"y_normed_{kk}"], at(f"y_normed_{kk}", bb, v))
                            mm = tokens(yhalf(s, t // 2)[:, (t % 2) * D:(t % 2 + 1) * D],
                                        lambda a, c: xt[k][a][:, c, t * P:(t + 1) * P],
                                        lambda w, c: w1[w][:, e, c, :], 0, e)
                            if t % 2:
                                mm.then_inc(sem[f"y_ready_{k}"], 1)
                    if i.live() and s == 0:
                        if (i - 1).live():
                            eng.wait_ge(sem["qk_rest"], at("qk_rest", i - 1))
                        gate_scores(i, "A", i)
                        if b_.live():
                            eng.wait_ge(sem["x_low_O"], at("x_low_O", b_))
                            project(i, b_)
                        gate_turn(i, "A", i)
                    if b_.live() and i.live() and s == step_gate(i, "B"):
                        eng.wait_ge(sem["x_low_B"], at("x_low_B", b_))
                        gate_scores(i, "B", b_)
                    if 1 <= s <= len(us):
                        k, b, e = us[s - 1]
                        eng.wait_ge(sem[f"y_normed_{k}"], at(f"y_normed_{k}", b, 2 * e + 2))
                        if s >= 2:
                            kk, bb, ee = us[s - 2]
                            eng.wait_ge(sem[f"h_high_{kk}"], at(f"h_high_{kk}", bb, 2 * ee + 2))
                        for c in range(C):
                            for t in range(T):
                                mm = eng.transpose(tps[:, c, t * P:(t + 1) * P], yn[:, t, c * P:(c + 1) * P],
                                                   identf[:, :])
                            mm.then_inc(sem[f"y_turned_{k}"], 1)
                    if b_.live() and i.live() and s == step_xb(i):
                        turn_b(i, b_)
                    if m.live() and early and s == len(us) + 1:
                        maxima(m, 1)
                    if s >= 2:
                        zstep(i, us, s - 2, (2, 3) if s == len(us) else (0, 1, 2, 3))
                    if m.live() and s == len(us):
                        eng.wait_ge(sem["stacks_placed"], at("stacks_placed", m))
                        if early:
                            maxima(m, 0)
                    if b_.live() and s == step_gate(i, "B"):
                        gate_turn(i, "B", b_)
                if i.live() and not b_.live():
                    k, b, e = us[-1]
                    eng.wait_ge(sem[f"h_high_{k}"], at(f"h_high_{k}", b))
                    xpose(i, "Q", i)
                for k, b, e in us[-2:]:
                    eng.wait_ge(sem[f"y_normed_{k}"], at(f"y_normed_{k}", b))
                    eng.wait_ge(sem[f"z_scaled_{k}"], at(f"z_scaled_{k}", b))
                if i.live():
                    eng.wait_ge(sem["x_low_Q"], at("x_low_Q", i))
                if m.live():
                    for h in range(2 if early else 0, LEAD):
                        maxima(m, h)
                for h in range(H):
                    if m.live() and h + LEAD < H:
                        maxima(m, h + LEAD)
                    if i.live() and h + LEAD >= H:
                        if m.live():
                            eng.wait_ge(sem["block_maxima"], at("block_maxima", m))
                        chunk(h + LEAD - H)
                    for p in range(2):
                        if e_.live():
                            if h:
                                eng.wait_ge(sem["exp_ready"], at("exp_ready", e_, 2 * h - 1 + p))
                            elif p == 0:
                                eng.wait_ge(sem["maxima_placed"], at("maxima_placed", e_))
                                eng.wait_ge(sem["v_copied"], at("v_copied", e_))
                            for j in EPART[p]:
                                o = ECOL[j]
                                w_ = S - j * P
                                eng.matmul(eps_[:, o:o + w_], ks[e_.s][0:KR + 3, h, j * P:(j + 1) * P],
                                           qs[e_.s][0:KR + 3, h, j * P:S], start=True, stop=False)
                                mm = eng.matmul(eps_[:, o:o + P], identb[:, :], mask_k[:, :], start=False, stop=True)
                            mm.then_inc(sem["keys_scored"], 1)
                    if e_.live():
                        if h % QUAD == 0 and h >= QUAD:
                            pv(e_, h // QUAD - 1)
                        if h % QUAD == 2 and h >= QUAD:
                            o_back(e_, h // QUAD - 1)
                nxt = Seq(i.n + 1, i.reg)

                if e_.live():
                    pv(e_, QUAD - 1)
                if i.live():
                    for t in range(T):
                        mm = tokens(bank[:, 3 + t // 2, (t % 2) * D:(t % 2 + 1) * D],
                                    lambda a, c: xt["Q"][a][:, c, t * P:(t + 1) * P],
                                    lambda w, c: wqkv[w][:, c, 2 * D:3 * D])
                        if t % 2:
                            mm.then_inc(sem["v_ready"], 1)
                if e_.live():
                    o_back(e_, QUAD - 1)
                if i.live():
                    chunk(2)
                    chunk(3)
                if m.live():
                    eng.wait_ge(sem["maxima_part"], at("maxima_part", m))
                    if e_.live():
                        eng.wait_ge(sem["pv_normed"], at("pv_normed", e_))
                    settled(eng)
                    r16 = rps.bitcast(bf16)
                    for t in range(T):
                        mm = eng.transpose(r16[0:3 * H, t * P:(t + 1) * P],
                                           nmp[:, t, :, :].rearrange("p a h -> p (a h)"), identb[:, :])
                    mm.then_inc(sem["maxima_turned"], 1)
                if nxt.live():
                    if i.live():
                        eng.wait_ge(sem["v_copied"], at("v_copied", i))
                    xpose(i, "A", nxt)
                if e_.live():
                    eng.wait_ge(sem["pv_normed"], at("pv_normed", e_))
                    if m.live():
                        eng.wait_ge(sem["maxima_copied"], at("maxima_copied", m))
                    for c in range(C):
                        for t in range(T):
                            mm = eng.transpose(xps(i, "O", c)[:, t * P:(t + 1) * P], on[:, t, c * P:(c + 1) * P],
                                               identf[:, :])
                        mm.then_inc(sem["x_turned_O"], 1)
                if i.live():
                    eng.wait_ge(sem["qk_rest"], at("qk_rest", i, 3))
                if e_.live() and not nxt.live():
                    eng.wait_ge(sem["x_low_O"], at("x_low_O", e_))
                if m.live():
                    eng.wait_ge(sem["maxima_copied"], at("maxima_copied", m))

            def pv(b, g):
                eng.wait_ge(sem["exp_ready"], at("exp_ready", b, 2 * (g + 1) * QUAD))
                if g:
                    eng.wait_ge(sem["pv_copied"], at("pv_copied", b, g))
                for j in range(T):
                    for q in range(QUAD):
                        h = g * QUAD + q
                        mm = eng.matmul(ops[q * 32:q * 32 + HD + 1, j * P:S], va[b.s][:, j, h, :],
                                        pt[:, h % NPT, ECOL[j]:ECOL[j] + S - j * P],
                                        start=(j == 0), stop=(j == T - 1))
                mm.then_inc(sem["pv_ready"], 1)

            def o_back(b, g):
                eng.wait_ge(sem["pv_copied"], at("pv_copied", b, g + 1))
                if g:
                    eng.wait_ge(sem["pv_normed"], at("pv_normed", b, g))
                for t in range(T):
                    mm = eng.transpose(rps[:, t * P:(t + 1) * P], ot[:, t * P:(t + 1) * P], identf[:, :])
                mm.then_inc(sem["pv_turned"], 1)

            xpose(Seq(0), "A", Seq(0))
            drive(eng, iteration)


_INS = ['L0_attn_x', 'L0_attn_Wq', 'L0_attn_Wkv', 'L0_attn_Wo', 'L0_ffn_gate_W', 'L0_ffn_gate_b', 'L0_ffn_W1',
        'L0_ffn_b1', 'L0_ffn_g1', 'L0_ffn_be1', 'L0_ffn_W2', 'L0_ffn_b2', 'L0_ffn_g2', 'L0_ffn_be2']


def kernel(**inputs):
    import numpy as _np
    import concourse.bacc as _bacc
    from concourse import mybir as _mybir
    from concourse.bass_utils import run_bass_kernel_spmd as _run

    nc = _bacc.Bacc("TRN2", target_bir_lowering=False, num_devices=1)
    arrays, args = {}, []
    for name in _INS:
        a = _np.ascontiguousarray(inputs[name])
        arrays[f"in_{name}_dram"] = a
        args.append(nc.dram_tensor(f"in_{name}_dram", a.shape, _mybir.dt.from_np(a.dtype), kind="ExternalInput").ap())
    shape = inputs['L0_attn_x'].shape
    args.append(nc.dram_tensor("out_0_dram", shape, _mybir.dt.float32, kind="ExternalOutput").ap())
    macaron_kernel(nc, *args)
    r = _run(nc, [arrays], core_ids=[0])
    return r.results[0]["out_0_dram"]
```

```python
import concourse.bass as bass
from concourse import mybir
from contextlib import ExitStack


def macaron_kernel(nc, x, Wq, Wkv, Wo, gate_W, gate_b, W1, b1, g1, be1, W2, b2, g2, be2, out):
    fp32, fp32r, bf16 = mybir.dt.float32, mybir.dt.float32r, mybir.dt.bfloat16
    ALU, ACT, AX = mybir.AluOpType, mybir.ActivationFunctionType, mybir.AxisListType

    NSEQ, S, D = x.shape
    NEXP = gate_W.shape[1]
    P = 128
    H, HD = 16, D // 16
    T = S // P
    C = D // P
    QUAD = 4
    SCALE = float(HD) ** -0.5
    LN_EPS = 1e-5
    MASKED = -1e30
    NBLK = T * (T + 1) // 2
    WIDE = NBLK * P
    QPART = (0, 0, 0, 1, 1, 2)
    KPART = (0, 1, 2, 0, 1, 0)
    G = len(QPART)
    KR = G * HD
    MCOL = {3: 0, 2: 4 * P, 0: 7 * P, 1: 8 * P}
    ECOL = {0: 0, 1: 4 * P, 3: 7 * P, 2: 8 * P}

    MPART = ((3,), (2, 0, 1))
    EPART = ((0,), (1, 3, 2))
    PCOL = (0, T * P, WIDE)
    SHIFT_AT = (10, 13, 14, 15)
    LEAD = 3

    ctx = ExitStack()
    with ctx:
        def sb(name, shape, dt=fp32):
            return ctx.enter_context(nc.sbuf_tensor(name, shape, dt))

        def ps(name, shape, dt=fp32):
            return ctx.enter_context(nc.psum_tensor(name, shape, dt))

        WKD = NEXP * C * D
        w1 = [sb(f"w1_{p}", [P, NEXP, C, D], fp32r) for p in "hl"]
        w2 = [sb(f"w2_{p}", [P, NEXP, C, D], fp32r) for p in "hl"]
        wqkv = [sb(f"wqkv_{p}", [P, C, 3 * D], fp32r) for p in "hl"]
        wo = [sb(f"wo_{p}", [P, C, D], fp32r) for p in "hl"]
        gw = [sb(f"gw_{p}", [P, C, NEXP], fp32r) for p in "hl"]
        gb = sb("gb", [NEXP, 1])
        BROWS, BSTEP = 96, 32
        bias = sb("bias", [BROWS, 2, D], bf16)
        rows_of = sb("rows_of", [BROWS, NEXP, P], bf16)
        g1c = sb("g1c", [P, NEXP, C])
        be1c = sb("be1c", [P, NEXP, C])
        g2b = sb("g2b", [P, NEXP, D])
        be2b = sb("be2b", [P, NEXP, D])
        identf = sb("identf", [P, P])
        identb = sb("identb", [P, P], bf16)
        mask_q = sb("mask_q", [P, P], bf16)
        mask_k = sb("mask_k", [P, P], bf16)
        neghalf = sb("neghalf", [P, 2 * T])
        lower = sb("lower", [P, T, NEXP, NEXP])
        acc = {k: sb(f"acc_{k}", [P, T, D]) for k in "AB"}
        xhat = sb("xhat", [P, T, D])
        on = sb("on", [P, T, D])
        xt = {k: [sb(f"xt{k}_{p}", [P, C, S], fp32r) for p in "hl"] for k in "AB"}
        xt["Q"], xt["O"] = xt["A"], xt["B"]
        mv = {k: sb(f"mv{k}", [P, T, 2]) for k in "ABQ"}
        st6 = {k: sb(f"st6{k}", [P, T, 6]) for k in "ABQ"}
        rstd = {k: sb(f"rstd{k}", [P, T]) for k in "ABQ"}
        rtmp = {k: sb(f"rtmp{k}", [P, T]) for k in "ABQ"}
        gs = {k: sb(f"gs{k}", [P, T, NEXP]) for k in "AB"}
        gmax = {k: sb(f"gmax{k}", [P, T]) for k in "AB"}
        gcmp = sb("gcmp", [P, T, NEXP, NEXP])
        gcmq = sb("gcmq", [P, T, NEXP, NEXP])
        grank = {k: sb(f"grank{k}", [P, T, NEXP]) for k in "AB"}
        gexp = {k: sb(f"gexp{k}", [P, T, NEXP]) for k in "AB"}
        gsum = {k: sb(f"gsum{k}", [P, T]) for k in "AB"}
        wgt = {k: sb(f"wgt{k}", [P, T, NEXP]) for k in "AB"}
        ss1 = {k: sb(f"ss1{k}", [P, T]) for k in "AB"}
        ss2 = {k: sb(f"ss2{k}", [P, T]) for k in "AB"}
        rs1 = {k: sb(f"rs1{k}", [P, T]) for k in "AB"}
        rs2 = {k: sb(f"rs2{k}", [P, T]) for k in "AB"}
        tmp1 = {k: sb(f"tmp1{k}", [P, T]) for k in "AB"}
        tmp2 = {k: sb(f"tmp2{k}", [P, T]) for k in "AB"}
        wst = {k: sb(f"wst{k}", [P, T]) for k in "AB"}
        junk = sb("junk", [P, T, D], bf16)
        hh = sb("hh", [P, C, S], fp32r)
        hl = sb("hl", [P, C, S], fp32r)
        qs = [sb(f"qs{s}", [P, H, S], bf16) for s in range(2)]
        ks = [sb(f"ks{s}", [P, H, S], bf16) for s in range(2)]
        va = [sb(f"va{s}", [P, T, H, HD + 1]) for s in range(2)]
        bm = sb("bm", [P, H, NBLK])
        nm = sb("nm", [P, T, H])
        nmr = sb("nmr", [P, T, H])
        nmp = sb("nmp", [P, T, 3, H], bf16)
        nmt = sb("nmt", [3 * H, S], bf16)
        ot = sb("ot", [P, S])
        rden = sb("rden", [P, T, QUAD])
        NPT = 5
        O_HF = T * D
        O_U = O_HF + C * S
        O_QK = O_U + T * D
        N_QK = 3 * C * S // 2
        O_G = O_QK + 2 * N_QK
        space = sb("space", [P, max(O_G + S, NPT * WIDE)])
        pt = space[:, 0:NPT * WIDE].rearrange("p (a n) -> p a n", a=NPT)
        yn = space[:, 0:O_HF].rearrange("p (t n) -> p t n", t=T)
        hf = space[:, O_HF:O_U].rearrange("p (c n) -> p c n", c=C)
        qkr = hf
        u = space[:, O_U:O_QK].rearrange("p (t n) -> p t n", t=T)
        res = u
        qkp = [space[:, O_QK + n * N_QK:O_QK + (n + 1) * N_QK].bitcast(bf16).rearrange(
            "p (a c s) -> p a c s", a=3, c=C) for n in range(2)]
        gt = space[0:NEXP, O_G:O_G + S]

        scratch = nc.dram_tensor("scratch", [2, 3, C, P, S], bf16, kind="Internal").ap()

        bank = ps("bank", [P, 8, 512])
        tps = bank[:, 3:5, :]
        mps = bank[:, 0:3, :].rearrange("p b n -> p (b n)")
        eps_ = bank[:, 3:6, :].rearrange("p b n -> p (b n)")
        ops = bank[:, 6, :]
        rps = bank[:, 7, :]
        mt = bank[:, 5, :]
        qkb = [bank[:, n, :] for n in (0, 1, 2, 5)]

        per = {}
        sem = {}

        def mk(name, n):
            per[name] = n
            sem[name] = ctx.enter_context(nc.semaphore(name))

        for k in "AB":
            mk(f"y_ready_{k}", 2 * NEXP)
            mk(f"y_squares_{k}", NEXP)
            mk(f"y_var_{k}", NEXP)
            mk(f"y_rstd_{k}", NEXP)
            mk(f"y_normed_{k}", 2 * NEXP)
            mk(f"y_turned_{k}", 2 * NEXP)
            mk(f"h_ready_{k}", 2 * NEXP)
            mk(f"h_high_{k}", 2 * NEXP)
            mk(f"h_low_{k}", 2 * NEXP)
            mk(f"z_ready_{k}", 2 * NEXP)
            mk(f"z_squares_{k}", NEXP)
            mk(f"z_var_{k}", NEXP)
            mk(f"z_rstd_{k}", NEXP)
            mk(f"z_factor_{k}", NEXP)
            mk(f"z_scaled_{k}", 2 * NEXP)
            mk(f"z_shifted_{k}", NEXP)
            mk(f"z_summed_{k}", NEXP)
            mk(f"sum_begun_{k}", 1)
            mk(f"gate_ready_{k}", 1)
            mk(f"gate_biased_{k}", 1)
            mk(f"gate_turned_{k}", 1)
            mk(f"gate_step_{k}", 10)
            mk(f"gate_reduced_{k}", 2)
            mk(f"gate_exp_{k}", 1)
        for k in "ABQ":
            mk(f"ln_stats_{k}", 1)
            mk(f"ln_parts_{k}", 1)
            mk(f"ln_var_{k}", 1)
            mk(f"ln_rstd_{k}", 1)
            mk(f"ln_ready_{k}", 1)
            mk(f"x_turned_{k}", C)
            mk(f"x_high_{k}", C)
            mk(f"x_low_{k}", C)
        mk("x_loaded", 16)
        mk("out_stored", 16)
        mk("x1_kept", 16)
        mk("x1_back", 16)
        mk("qk_ready", 2 * C)
        mk("qk_part1", 2 * C)
        mk("qk_rest", 2 * C)
        mk("qk_part2", 2 * C)
        mk("qk_part3", 2 * C)
        mk("v_ready", 2)
        mk("v_copied", 2)
        mk("parts_stored", 16 * 2)
        mk("stacks_placed", 16 * 2 * G)
        mk("queries_scored", 2 * H)
        mk("block_maxima", 2 * H)
        mk("maxima_ready", 1)
        mk("maxima_part", 3)
        mk("maxima_rest", 2)
        mk("maxima_turned", 1)
        mk("maxima_copied", 1)
        mk("maxima_placed", 16 * 3)
        mk("keys_scored", 2 * H)
        mk("exp_ready", 2 * H)
        mk("pv_ready", QUAD)
        mk("pv_copied", QUAD)
        mk("pv_turned", QUAD)
        mk("sums_inverted", QUAD)
        mk("pv_normed", QUAD)
        mk("x_turned_O", C)
        mk("x_high_O", C)
        mk("x_low_O", C)
        mk("wo_ready", 2)
        mk("attention_added", 1)
        for n in ("first_x_loaded", "w1_loaded", "small_loaded", "weights_loaded", "pool_setup", "dve_setup",
                  "act_setup", "settled"):
            mk(n, 0)

        class Seq:

            def __init__(self, n, reg=None):
                self.n, self.reg = n, reg
                self.s = n % 2

            def __sub__(self, k):
                return Seq(self.n - k, self.reg)

            def live(self):
                return self.reg is not None or 0 <= self.n < NSEQ

        def at(name, b, k=None):
            n = per[name]
            v = b.n * n + (n if k is None else k)
            if b.reg is None:
                return max(0, min(v, NSEQ * n))
            assert v > 0, name
            return b.reg * (2 * n) + v

        def settled(eng):
            eng.sem_inc(sem["settled"], 1)

        def units(i):
            return [(k, q, e) for k, q in (("A", i), ("B", i - 3)) if q.live() for e in range(NEXP)]

        def yhalf(s, j):
            return bank[:, (2 * s + j) % 3, :]

        def rotation(i):
            a, b = i, i - 3
            us = units(i)
            order = []
            for s in range(len(us) + 2):
                for k, q in (("A", a), ("B", b)):
                    if k == "B" and q.live() and s == 0:
                        order += [(("wo", j), ("attention_added", b, 1)) for j in range(2)]
                    if k == "B" and q.live() and s == step_xb(i):
                        order += [(("x", c), ("x_low_B", b, c + 1)) for c in range(C)]
                    if q.live() and s == step_gate(i, k):
                        order.append((("gate", k), (f"gate_step_{k}", q, 1)))
                if s >= 2:
                    k, q, e = us[s - 2]
                    order += [(("z", s - 2, j), (f"z_scaled_{k}", q, 2 * e + j + 1)) for j in range(2)]
            return order

        def place(i, *user):
            order = rotation(i)
            n = [u_ for u_, _ in order].index(user)
            return bank[:, 5 + n % 3, :], (order[n - 3][1] if n >= 3 else None)

        def xps(i, k, c):
            if k == "O":
                return bank[:, 6 + c, :]
            if k == "B":
                return place(i, "x", c)[0]
            return tps[:, c, :]

        def step_xb(i):
            return 3 if i.live() else 0

        def step_gate(i, k):
            return NEXP if k == "B" and i.live() else 0

        def step_q(i):
            return len(units(i)) + (1 if (i - 3).live() else 2)

        st_a = qs[0][:, :, :].rearrange("p h s -> p (h s)").bitcast(fp32)
        st_c = qs[1][:, :, :].rearrange("p h s -> p (h s)").bitcast(fp32)
        SWO = C * 3 * D
        SG = SWO + C * D
        st_w1, st_w2 = st_a[:, 0:WKD], st_a[:, WKD:2 * WKD]
        st_qkv, st_wo, st_g = st_c[:, 0:SWO], st_c[:, SWO:SG], st_c[:, SG:SG + C * NEXP]
        st_b = on[0:BROWS, 0:2, :]
        bpart = on[0:BROWS, 2, :].bitcast(bf16).rearrange("p (m n) -> p m n", m=2)
        rowsum = sb("rowsum", [P, 2, NEXP * C])
        bsum = sb("bsum", [BROWS, 2])
        expert_row = sb("expert_row", [BROWS, NEXP])

        def drive(eng, iteration):
            first = 4
            loops = max(NSEQ - 1 - first, 0) // 2
            for i in range(min(first, NSEQ + 3)):
                iteration(Seq(i))
            if loops:
                with eng.Fori(0, loops) as r:
                    for o in range(2):
                        iteration(Seq(first + o, r))
            for i in range(first + 2 * loops, NSEQ + 3):
                iteration(Seq(i))

        NSMALL = 2 + 6 + 2 * C
        NREST = 6
        NPOOL_FIRST = 3
        NPOOL = NPOOL_FIRST + 5 + NEXP + 4
        NDVE_W1, NDVE_FIRST = 4, 21
        NDVE = NDVE_FIRST + 6

        block = ctx.enter_context(nc.Block())

        @block.sync
        def _(eng):
            def load(done, dst, src):
                eng.dma_start(dst, src, allow_slow_non_contiguous=True).then_inc(sem[done], 16)

            load("first_x_loaded", acc["A"][:, :, :], x[0, :, :].rearrange("(t p) d -> p t d", p=P))
            load("w1_loaded", st_w1.rearrange("p (a n) -> p a n", n=D), W1.rearrange("e (c p) n -> p (e c) n", p=P))
            load("small_loaded", st_g.rearrange("p (c n) -> p c n", c=C), gate_W.rearrange("(c p) n -> p c n", p=P))
            load("small_loaded", gb[:, :], gate_b.rearrange("(n o) -> n o", o=1))
            eng.wait_ge(sem["dve_setup"], 1)
            for m, b in enumerate((b1, b2)):
                for r in range(3):
                    load("small_loaded", on[r * BSTEP:r * BSTEP + NEXP, m, :], b)
            for c in range(C):
                load("small_loaded", g1c[:, :, c], g1[:, c * P:(c + 1) * P].rearrange("e p -> p e"))
                load("small_loaded", be1c[:, :, c], be1[:, c * P:(c + 1) * P].rearrange("e p -> p e"))
            load("weights_loaded", st_w2.rearrange("p (a n) -> p a n", n=D), W2.rearrange("e (c p) n -> p (e c) n", p=P))
            load("weights_loaded", st_qkv.rearrange("p (c n) -> p c n", c=C)[:, :, 0:D],
                 Wq.rearrange("(c p) n -> p c n", p=P))
            load("weights_loaded", st_qkv.rearrange("p (c n) -> p c n", c=C)[:, :, D:3 * D],
                 Wkv.rearrange("(c p) n -> p c n", p=P))
            load("weights_loaded", st_wo.rearrange("p (c n) -> p c n", c=C), Wo.rearrange("(c p) n -> p c n", p=P))
            for dst, src in ((g2b, g2), (be2b, be2)):
                load("weights_loaded", dst[:, :, :].rearrange("p e n -> p (e n)"),
                     src.rearrange("(o e) n -> o (e n)", o=1).broadcast_to([P, NEXP * D]))

            def rows(t, b):
                v = t[b.n, :, :] if b.reg is None else \
                    t[bass.ds(b.reg * 2 + b.n, 1), :, :].rearrange("o s d -> (o s) d")
                return v.rearrange("(t p) d -> p t d", p=P)

            def iteration(i):
                b = i
                if b.live():
                    eng.wait_ge(sem["z_summed_A"], at("z_summed_A", b))
                    settled(eng)
                    eng.dma_start(rows(out, b), acc["A"][:, :, :]).then_inc(sem["x1_kept"], 16)
                b = Seq(i.n + 1, i.reg)
                if b.live():
                    eng.wait_ge(sem["x1_kept"], at("x1_kept", i))
                    settled(eng)
                    eng.wait_ge(sem["ln_ready_Q"], at("ln_ready_Q", i))
                    settled(eng)
                    eng.dma_start(acc["A"][:, :, :], rows(x, b)).then_inc(sem["x_loaded"], 16)
                b = i - 3
                if b.live():
                    eng.wait_ge(sem["z_shifted_B"], at("z_shifted_B", b))
                    settled(eng)
                    eng.dma_start(rows(out, b), acc["B"][:, :, :]).then_inc(sem["out_stored"], 16)
                b = i - 2
                if b.live():
                    eng.wait_ge(sem["x1_kept"], at("x1_kept", b))
                    settled(eng)
                    eng.wait_ge(sem["attention_added"], at("attention_added", b - 1))
                    settled(eng)
                    eng.wait_ge(sem["pv_ready"], at("pv_ready", b))
                    settled(eng)
                    eng.dma_start(res[:, :, :], rows(out, b)).then_inc(sem["x1_back"], 16)
                b = i - 1
                if b.live():
                    eng.wait_ge(sem["maxima_copied"], at("maxima_copied", b))
                    settled(eng)
                    for p in range(3):
                        eng.dma_start(qs[b.s][KR + p:KR + p + 1, :, :], nmt[p * H:(p + 1) * H, :]).then_inc(sem["maxima_placed"], 16)
                b = i
                if b.live():
                    eng.wait_ge(sem["stacks_placed"], at("stacks_placed", b - 1))
                    settled(eng)
                    for n_ in range(2):
                        eng.wait_ge(sem["qk_part3"], at("qk_part3", b, C * (n_ + 1)))
                        settled(eng)
                        eng.dma_start(scratch[n_, :, :, :, :].rearrange("a c p s -> p a c s"),
                                      qkp[n_]).then_inc(sem["parts_stored"], 16)
                    eng.wait_ge(sem["keys_scored"], at("keys_scored", b - 2))
                    settled(eng)
                    for n_, (dst, part) in enumerate(((qs, QPART), (ks, KPART))):
                        eng.wait_ge(sem["parts_stored"], at("parts_stored", b))
                        settled(eng)
                        for g in range(G):
                            eng.dma_start(dst[b.s][g * HD:(g + 1) * HD, :, :],
                                          scratch[n_, part[g], :, :, :].rearrange("c (hc d) s -> d (c hc) s", d=HD)
                                          ).then_inc(sem["stacks_placed"], 16)

            drive(eng, iteration)
            eng.wait_ge(sem["out_stored"], at("out_stored", Seq(NSEQ - 1)))
            eng.wait_ge(sem["x_loaded"], at("x_loaded", Seq(NSEQ - 2)))
            eng.wait_ge(sem["stacks_placed"], at("stacks_placed", Seq(NSEQ - 1)))


        @block.gpsimd
        def _(eng):
            cp = [0]

            def step(ins):
                cp[0] += 1
                ins.then_inc(sem["pool_setup"], 1)
                eng.wait_ge(sem["pool_setup"], cp[0])

            step(eng.memset(identf[:, :], 0.0))
            step(eng.affine_select(out=identf[:, :], in_=identf[:, :], compare_op=ALU.not_equal, fill=1.0,
                                   base=0, pattern=[[-1, P]], channel_multiplier=1))
            step(eng.memset(neghalf[:, :], -0.5))
            assert cp[0] == NPOOL_FIRST

            def rest_of_setup():
                step(eng.tensor_copy(identb[:, :], identf[:, :]))
                step(eng.memset(mask_q[:, :], 0.0))
                step(eng.affine_select(out=mask_q[:, :], in_=mask_q[:, :], compare_op=ALU.is_ge, fill=MASKED,
                                       base=0, pattern=[[-1, P]], channel_multiplier=1))
                step(eng.memset(mask_k[:, :], 0.0))
                step(eng.affine_select(out=mask_k[:, :], in_=mask_k[:, :], compare_op=ALU.is_ge, fill=MASKED,
                                       base=0, pattern=[[1, P]], channel_multiplier=-1))
                step(eng.memset(lower[:, :, :, :], 0.0))
                for e in range(1, NEXP):
                    step(eng.memset(lower[:, :, e, 0:e], 1.0))
                for s in range(2):
                    step(eng.memset(va[s][:, :, :, HD:HD + 1], 1.0))
                    step(eng.memset(ks[s][64:P, :, :], 1.0))
                assert cp[0] == NPOOL, (cp, NPOOL)

            def ln(k, b):
                eng.wait_ge(sem[f"ln_stats_{k}"], at(f"ln_stats_{k}", b))
                settled(eng)
                eng.tensor_scalar(rtmp[k][:, :], mv[k][:, :, 1], LN_EPS, None, ALU.add).then_inc(sem[f"ln_var_{k}"], 1)
                eng.wait_ge(sem[f"ln_var_{k}"], at(f"ln_var_{k}", b))
                eng.tensor_tensor(rstd[k][:, :], rtmp[k][:, :], neghalf[:, 0:T], ALU.pow).then_inc(sem[f"ln_rstd_{k}"], 1)

            def iteration(i):
                us = units(i)
                b_ = i - 3
                for s in range(len(us) + 3):
                    if b_.live() and s == (1 if i.live() else 0):
                        ln("B", b_)
                    if s < len(us):
                        k, b, e = us[s]
                        eng.wait_ge(sem[f"y_squares_{k}"], at(f"y_squares_{k}", b, e + 1))
                        eng.wait_ge(sem[f"y_normed_{k}"], at(f"y_normed_{k}", b, 2 * e))
                        settled(eng)
                        eng.tensor_scalar(tmp1[k][:, :], ss1[k][:, :], 1.0 / D, LN_EPS, ALU.mult,
                                          ALU.add).then_inc(sem[f"y_var_{k}"], 1)
                        eng.wait_ge(sem[f"y_var_{k}"], at(f"y_var_{k}", b, e + 1))
                        eng.tensor_tensor(rs1[k][:, :], tmp1[k][:, :], neghalf[:, 0:T],
                                          ALU.pow).then_inc(sem[f"y_rstd_{k}"], 1)
                    if i.live() and b_.live() and s == step_q(i) - 2:
                        ln("Q", i)
                    if s >= 3:
                        k, b, e = us[s - 3]
                        if k == "A":
                            eng.wait_ge(sem["z_shifted_A"], at("z_shifted_A", b, e + 1))
                        elif e == 0:
                            eng.wait_ge(sem["sum_begun_B"], at("sum_begun_B", b))
                        else:
                            eng.wait_ge(sem["z_summed_B"], at("z_summed_B", b, e))
                        eng.wait_ge(sem[f"z_scaled_{k}"], at(f"z_scaled_{k}", b, 2 * e + 2))
                        eng.tensor_tensor(acc[k][:, :, :], acc[k][:, :, :], u[:, :, :], ALU.add).then_inc(sem[f"z_summed_{k}"], 1)
                    if 2 <= s < len(us) + 2:
                        k, b, e = us[s - 2]
                        eng.wait_ge(sem[f"z_squares_{k}"], at(f"z_squares_{k}", b, e + 1))
                        if e == 0:
                            eng.wait_ge(sem[f"gate_step_{k}"], at(f"gate_step_{k}", b))
                        settled(eng)
                        eng.tensor_scalar(tmp2[k][:, :], ss2[k][:, :], 1.0 / D, LN_EPS, ALU.mult,
                                          ALU.add).then_inc(sem[f"z_var_{k}"], 1)
                        eng.wait_ge(sem[f"z_var_{k}"], at(f"z_var_{k}", b, e + 1))
                        eng.tensor_tensor(rs2[k][:, :], tmp2[k][:, :], neghalf[:, 0:T],
                                          ALU.pow).then_inc(sem[f"z_rstd_{k}"], 1)
                        eng.wait_ge(sem[f"z_rstd_{k}"], at(f"z_rstd_{k}", b, e + 1))
                        eng.wait_ge(sem[f"z_scaled_{k}"], at(f"z_scaled_{k}", b, 2 * e))
                        eng.tensor_tensor(wst[k][:, :], rs2[k][:, :], wgt[k][:, :, e], ALU.mult).then_inc(sem[f"z_factor_{k}"], 1)
                if i.live() and not b_.live():
                    ln("Q", i)
                if Seq(i.n + 1, i.reg).live():
                    ln("A", Seq(i.n + 1, i.reg))
                if i.live():
                    for n_ in range(2 * C):
                        eng.wait_ge(sem["qk_part2"], at("qk_part2", i, n_ + 1))
                        eng.tensor_tensor(qkp[n_ // C][:, 2, n_ % C, :], qkr[:, n_ % 2, :],
                                              qkp[n_ // C][:, 1, n_ % C, :], ALU.subtract).then_inc(sem["qk_part3"], 1)

            ln("A", Seq(0))
            rest_of_setup()
            drive(eng, iteration)


        @block.scalar
        def _(eng):
            def high(i, k, b):
                for c in range(C):
                    eng.wait_ge(sem[f"x_turned_{k}"], at(f"x_turned_{k}", b, c + 1))
                    eng.activation(xt[k][0][:, c, :], xps(i, k, c), ACT.Copy).then_inc(sem[f"x_high_{k}"], 1)

            def squares(i, us, s):
                if s >= 2:
                    k, b, e = us[s - 2]
                    eng.wait_ge(sem[f"z_var_{k}"], at(f"z_var_{k}", b, e))
                    if s < len(us):
                        eng.wait_ge(sem[f"y_squares_{us[s][0]}"], at(f"y_squares_{us[s][0]}", us[s][1], us[s][2] + 1))
                    else:
                        kk, bb, ee = us[s - 3] if s > 2 else us[-1]
                        eng.wait_ge(sem[f"z_squares_{kk}" if s > 2 else f"y_squares_{kk}"], at(f"z_squares_{kk}" if s > 2 else f"y_squares_{kk}", bb, ee + 1))
                        eng.wait_ge(sem[f"y_squares_{us[-1][0]}"], at(f"y_squares_{us[-1][0]}", us[-1][1]))
                    for t in range(T):
                        if t % 2 == 0:
                            eng.wait_ge(sem[f"z_ready_{k}"], at(f"z_ready_{k}", b, 2 * e + t // 2 + 1))
                        ins = eng.activation(junk[:, t, :], place(i, "z", s - 2, t // 2)[0][:, (t % 2) * D:(t % 2 + 1) * D],
                                             ACT.Square, accum_out=ss2[k][:, t:t + 1])
                    ins.then_inc(sem[f"z_squares_{k}"], 1)

            def high_h(i, us, s):
                if 1 <= s <= len(us):
                    k, b, e = us[s - 1]
                    if s >= 2:
                        kk, bb, ee = us[s - 2]
                        eng.wait_ge(sem[f"z_ready_{kk}"], at(f"z_ready_{kk}", bb, 2 * ee + 2))
                    for c in range(C):
                        eng.activation(hh[:, c, :], tps[:, c, :], ACT.Relu,
                                       bias=be1c[:, e, c:c + 1], scale=g1c[:, e, c:c + 1]).then_inc(sem[f"h_high_{k}"], 1)

            def iteration(i):
                us = units(i)
                b_ = i - 3
                for s in range(len(us) + 2):
                    if b_.live() and not i.live() and s == 0:
                        high(i, "B", b_)
                    if i.live() and b_.live() and s == step_q(i):
                        high(i, "Q", i)
                    if s < len(us):
                        k, b, e = us[s]
                        eng.wait_ge(sem[f"y_var_{k}"], at(f"y_var_{k}", b, e))
                        if s:
                            kk, bb, ee = us[s - 1]
                            eng.wait_ge(sem[f"y_squares_{kk}"], at(f"y_squares_{kk}", bb, ee + 1))
                            if s > 2:
                                kk, bb, ee = us[s - 3]
                                eng.wait_ge(sem[f"z_squares_{kk}"], at(f"z_squares_{kk}", bb, ee + 1))
                        else:
                            for kk, bb in (("A", i - 1), ("B", i - 4)):
                                if bb.live():
                                    eng.wait_ge(sem[f"z_squares_{kk}"], at(f"z_squares_{kk}", bb))
                        for t in range(T):
                            if t % 2 == 0:
                                eng.wait_ge(sem[f"y_ready_{k}"], at(f"y_ready_{k}", b, 2 * e + t // 2 + 1))
                            ins = eng.activation(junk[:, t, :], yhalf(s, t // 2)[:, (t % 2) * D:(t % 2 + 1) * D],
                                                 ACT.Square, accum_out=ss1[k][:, t:t + 1])
                        ins.then_inc(sem[f"y_squares_{k}"], 1)
                    if b_.live() and i.live() and s == step_xb(i):
                        high(i, "B", b_)
                    for k, b in (("A", i), ("B", b_)):
                        if b.live() and s == step_gate(i, k) + 1:
                            eng.wait_ge(sem[f"gate_step_{k}"], at(f"gate_step_{k}", b, 2))
                            eng.activation(gexp[k][:, :, :], gcmp[:, :, 0, :], ACT.Exp).then_inc(sem[f"gate_exp_{k}"], 1)
                    if 1 <= s <= len(us):
                        k, b, e = us[s - 1]
                        if s == 1 and (i - 1).live():
                            eng.wait_ge(sem["qk_part3"], at("qk_part3", i - 1))
                        if s >= 2:
                            kk, bb, ee = us[s - 2]
                            eng.wait_ge(sem[f"h_low_{kk}"], at(f"h_low_{kk}", bb, 2 * ee + 2))
                        for c in range(C):
                            eng.wait_ge(sem[f"y_turned_{k}"], at(f"y_turned_{k}", b, 2 * e + c + 1))
                            eng.activation(hf[:, c, :], tps[:, c, :], ACT.Relu,
                                               bias=be1c[:, e, c:c + 1], scale=g1c[:, e, c:c + 1]).then_inc(sem[f"h_ready_{k}"], 1)
                    squares(i, us, s)
                    high_h(i, us, s)
                if i.live() and not b_.live():
                    high(i, "Q", i)
                m, e_ = i - 1, i - 2
                if e_.live():
                    for h in range(H):
                        if h == 0:
                            for k, b in (("A", i), ("B", i - 3)):
                                if b.live():
                                    eng.wait_ge(sem[f"z_summed_{k}"], at(f"z_summed_{k}", b))
                            eng.wait_ge(sem["parts_stored"], at("parts_stored", i - 1))
                        if h >= NPT:
                            eng.wait_ge(sem["pv_ready"], at("pv_ready", e_, (h - NPT) // QUAD + 1))
                        for p in range(2):
                            eng.wait_ge(sem["keys_scored"], at("keys_scored", e_, 2 * h + p + 1))
                            eng.activation(pt[:, h % NPT, PCOL[p]:PCOL[p + 1]], eps_[:, PCOL[p]:PCOL[p + 1]], ACT.Exp,
                                           scale=SCALE).then_inc(sem["exp_ready"], 1)
                        if h % QUAD == 1 and h >= QUAD:
                            o_copy(e_, h // QUAD - 1)
                    o_copy(e_, QUAD - 1)
                nxt = Seq(i.n + 1, i.reg)

                def parts(n0):
                    for n_ in (n0, n0 + 1):
                        eng.wait_ge(sem["qk_ready"], at("qk_ready", i, n_ + 1))
                        if n_ == 0:
                            eng.wait_ge(sem["parts_stored"], at("parts_stored", i - 1))
                        eng.activation(qkp[n_ // C][:, 0, n_ % C, :], qkb[n_], ACT.Copy).then_inc(sem["qk_part1"], 1)

                def second(n0):
                    for n_ in (n0, n0 + 1):
                        eng.wait_ge(sem["qk_rest"], at("qk_rest", i, n_ + 1))
                        eng.activation(qkp[n_ // C][:, 1, n_ % C, :], qkr[:, n_ % 2, :], ACT.Copy).then_inc(sem["qk_part2"], 1)

                if m.live():
                    eng.wait_ge(sem["maxima_turned"], at("maxima_turned", m))
                    eng.wait_ge(sem["maxima_placed"], at("maxima_placed", m - 1))
                    eng.activation(nmt[:, :], mt.bitcast(bf16)[0:3 * H, 0:S], ACT.Copy).then_inc(sem["maxima_copied"], 1)
                if i.live():
                    parts(0)
                    second(0)
                if nxt.live():
                    high(i, "A", nxt)
                if i.live():
                    parts(2)
                if e_.live():
                    high(i, "O", e_)
                if i.live():
                    second(2)

            def o_copy(b, g):
                eng.wait_ge(sem["pv_ready"], at("pv_ready", b, g + 1))
                eng.wait_ge(sem["pv_turned"], at("pv_turned", b, g))
                eng.activation(ot[:, :], ops, ACT.Copy).then_inc(sem["pv_copied"], 1)

            def high_weights(w, st):
                w_ = w[0]
                flat = w_[:, :, :, :].rearrange("p e c n -> p (e c n)") if len(w_.shape) == 4 else \
                    w_[:, :, :].rearrange("p c n -> p (c n)")
                eng.activation(flat, st, ACT.Copy).then_inc(sem["act_setup"], 1)

            eng.wait_ge(sem["w1_loaded"], 16)
            eng.wait_ge(sem["dve_setup"], NDVE_W1)
            high_weights(w1, st_w1)
            high(Seq(0), "A", Seq(0))
            eng.wait_ge(sem["weights_loaded"], 16 * NREST)
            high_weights(wqkv, st_qkv)
            high_weights(wo, st_wo)
            eng.wait_ge(sem["dve_setup"], NDVE_FIRST + 3)
            high_weights(w2, st_w2)
            drive(eng, iteration)

        @block.vector
        def _(eng):
            cd = [0]

            def step(ins):
                cd[0] += 1
                ins.then_inc(sem["dve_setup"], 1)
                eng.wait_ge(sem["dve_setup"], cd[0])

            def centre(m, st):
                v = st.rearrange("p (a n) -> p a n", n=D)
                step(eng.tensor_reduce(rowsum[:, m, :], v, AX.X, ALU.add))
                step(eng.tensor_scalar(rowsum[:, m, :], rowsum[:, m, :], -1.0 / D, None, ALU.mult))
                step(eng.tensor_tensor(v, v, rowsum[:, m, :].unsqueeze(2).broadcast_to([P, NEXP * C, D]), ALU.add))

            def low_weights(w, st):
                flat = [w_[:, :, :, :].rearrange("p e c n -> p (e c n)") if len(w_.shape) == 4 else
                        w_[:, :, :].rearrange("p c n -> p (c n)") for w_ in w]
                step(eng.tensor_tensor(flat[1], st, flat[0].bitcast(fp32), ALU.subtract))

            def first_setup():
                eng.wait_ge(sem["w1_loaded"], 16)
                centre(0, st_w1)
                assert cd[0] == NDVE_W1

            def second_setup():
                eng.wait_ge(sem["small_loaded"], 16 * NSMALL)
                step(eng.tensor_reduce(bsum[:, :], st_b, AX.X, ALU.add))
                step(eng.tensor_scalar(bsum[:, :], bsum[:, :], -1.0 / D, None, ALU.mult))
                step(eng.tensor_tensor(st_b, st_b, bsum[:, :].unsqueeze(2).broadcast_to([BROWS, 2, D]), ALU.add))
                for r in range(3):
                    rr = slice(r * BSTEP, (r + 1) * BSTEP)
                    step(eng.tensor_copy(bpart, st_b))
                    if r < 2:
                        step(eng.tensor_tensor(st_b, st_b, bpart, ALU.subtract))
                    step(eng.tensor_copy(bias[rr, :, :], bpart[rr, :, :]))
                step(eng.tensor_tensor(expert_row[:, :], identf[0:BROWS, 0:NEXP], identf[0:BROWS, BSTEP:BSTEP + NEXP],
                                       ALU.add))
                step(eng.tensor_tensor(expert_row[:, :], expert_row[:, :],
                                       identf[0:BROWS, 2 * BSTEP:2 * BSTEP + NEXP], ALU.add))
                step(eng.tensor_copy(rows_of[:, :, :], expert_row[:, :].unsqueeze(2).broadcast_to([BROWS, NEXP, P])))
                step(eng.tensor_copy(gw[0][:, :, :].rearrange("p c n -> p (c n)"), st_g))
                low_weights(gw, st_g)
                eng.wait_ge(sem["act_setup"], 1)
                low_weights(w1, st_w1)
                assert cd[0] == NDVE_FIRST, cd

            def rest_of_setup():
                eng.wait_ge(sem["weights_loaded"], 16 * NREST)
                centre(1, st_w2)
                eng.wait_ge(sem["act_setup"], 3)
                low_weights(wqkv, st_qkv)
                low_weights(wo, st_wo)
                eng.wait_ge(sem["act_setup"], 4)
                low_weights(w2, st_w2)
                assert cd[0] == NDVE, cd

            def ln(k, b, src):
                for t in range(T):
                    ins = eng.bn_stats(out=st6[k][:, t, :], in_=src[:, t, :])
                ins.then_inc(sem[f"ln_parts_{k}"], 1)
                eng.wait_ge(sem[f"ln_parts_{k}"], at(f"ln_parts_{k}", b))
                settled(eng)
                for t in range(T):
                    ins = eng.bn_aggr(out=mv[k][:, t, :], in_=st6[k][:, t, :])
                ins.then_inc(sem[f"ln_stats_{k}"], 1)

            def ln_out(k, b, src):
                eng.wait_ge(sem[f"ln_rstd_{k}"], at(f"ln_rstd_{k}", b))
                for t in range(T):
                    ins = eng.tensor_scalar(xhat[:, t, :], src[:, t, :], mv[k][:, t, 0:1], rstd[k][:, t:t + 1],
                                            ALU.subtract, ALU.mult)
                ins.then_inc(sem[f"ln_ready_{k}"], 1)

            def begin(k, b):
                eng.wait_ge(sem[f"ln_ready_{k}"], at(f"ln_ready_{k}", b))
                eng.scalar_tensor_tensor(out=acc[k][:, :, :], in0=xhat[:, :, :], scalar=0.5, in1=acc[k][:, :, :],
                                         op0=ALU.mult, op1=ALU.add).then_inc(sem[f"sum_begun_{k}"], 1)

            def biased(i, k, b):
                eng.wait_ge(sem[f"gate_ready_{k}"], at(f"gate_ready_{k}", b))
                eng.tensor_scalar(gt, place(i, "gate", k)[0][0:NEXP, :], gb[:, 0:1], None,
                                  ALU.add).then_inc(sem[f"gate_biased_{k}"], 1)

            def add_attention(i, b):
                eng.wait_ge(sem["x1_back"], at("x1_back", b))
                eng.wait_ge(sem["out_stored"], at("out_stored", b - 1))
                for j in range(2):
                    eng.wait_ge(sem["wo_ready"], at("wo_ready", b, j + 1))
                    ins = eng.tensor_tensor(acc["B"][:, 2 * j:2 * j + 2, :],
                                            place(i, "wo", j)[0].rearrange("p (t n) -> p t n", t=2),
                                            res[:, 2 * j:2 * j + 2, :], ALU.add)
                ins.then_inc(sem["attention_added"], 1)
                eng.wait_ge(sem["attention_added"], at("attention_added", b))
                ln("B", b, acc["B"])

            def low(i, k, b):
                for c in range(C):
                    eng.wait_ge(sem[f"x_high_{k}"], at(f"x_high_{k}", b, c + 1))
                    eng.tensor_tensor(xt[k][1][:, c, :], xps(i, k, c), xt[k][0][:, c, :].bitcast(fp32),
                                          ALU.subtract).then_inc(sem[f"x_low_{k}"], 1)

            def gate_step(k, b, n, ins):
                ins.then_inc(sem[f"gate_step_{k}"], 1)
                eng.wait_ge(sem[f"gate_step_{k}"], at(f"gate_step_{k}", b, n))

            def gate_scores(i, k, b):
                eng.wait_ge(sem[f"gate_turned_{k}"], at(f"gate_turned_{k}", b))
                gate_step(k, b, 1, eng.tensor_copy(gs[k][:, :, :], place(i, "gate", k)[0][:, 0:T * NEXP].rearrange("p (t e) -> p t e", e=NEXP)))
                eng.tensor_reduce(gmax[k][:, :], gs[k][:, :, :], AX.X, ALU.max).then_inc(sem[f"gate_reduced_{k}"], 1)
                eng.wait_ge(sem[f"gate_reduced_{k}"], at(f"gate_reduced_{k}", b, 1))
                eng.tensor_tensor(gcmp[:, :, 0, :], gs[k][:, :, :],
                                  gmax[k][:, :].unsqueeze(2).broadcast_to([P, T, NEXP]),
                                  ALU.subtract).then_inc(sem[f"gate_step_{k}"], 1)

            def gate_weights(k, b):
                mine = gs[k][:, :, :].unsqueeze(3).broadcast_to([P, T, NEXP, NEXP])
                other = gs[k][:, :, :].unsqueeze(2).broadcast_to([P, T, NEXP, NEXP])
                eng.wait_ge(sem[f"gate_exp_{k}"], at(f"gate_exp_{k}", b))
                gate_step(k, b, 3, eng.tensor_tensor(gcmp[:, :, :, :], other, mine, ALU.is_gt))
                gate_step(k, b, 4, eng.tensor_tensor(gcmq[:, :, :, :], other, mine, ALU.is_equal))
                gate_step(k, b, 5, eng.tensor_tensor(gcmq[:, :, :, :], gcmq[:, :, :, :], lower[:, :, :, :], ALU.mult))
                gate_step(k, b, 6, eng.tensor_tensor(gcmp[:, :, :, :], gcmp[:, :, :, :], gcmq[:, :, :, :], ALU.add))
                gate_step(k, b, 7, eng.tensor_reduce(grank[k][:, :, :], gcmp[:, :, :, :], AX.X, ALU.add))
                gate_step(k, b, 8, eng.scalar_tensor_tensor(out=gexp[k][:, :, :], in0=grank[k][:, :, :], scalar=1.5,
                                                       in1=gexp[k][:, :, :], op0=ALU.is_lt, op1=ALU.mult))
                eng.tensor_reduce(gsum[k][:, :], gexp[k][:, :, :], AX.X, ALU.add).then_inc(sem[f"gate_reduced_{k}"], 1)
                eng.wait_ge(sem[f"gate_reduced_{k}"], at(f"gate_reduced_{k}", b, 2))
                gate_step(k, b, 9, eng.reciprocal(gsum[k][:, :], gsum[k][:, :]))
                gate_step(k, b, 10, eng.scalar_tensor_tensor(out=wgt[k][:, :, :], in0=gexp[k][:, :, :], scalar=0.5,
                                                        in1=gsum[k][:, :].unsqueeze(2).broadcast_to([P, T, NEXP]),
                                                        op0=ALU.mult, op1=ALU.mult))

            def iteration(i):
                us = units(i)
                b_ = i - 3
                nxt = Seq(i.n + 1, i.reg)
                m, e_ = i - 1, i - 2
                early = b_.live() or not i.live()
                for s in range(len(us) + 2):
                    if b_.live() and not i.live() and s == 0:
                        add_attention(i, b_)
                        ln_out("B", b_, acc["B"])
                        begin("B", b_)
                        low(i, "B", b_)
                    for k, b in (("A", i), ("B", b_)):
                        if b.live() and s == step_gate(i, k):
                            biased(i, k, b)
                    if b_.live() and i.live() and s == step_xb(i):
                        low(i, "B", b_)
                    if b_.live() and i.live() and s == 1:
                        eng.wait_ge(sem["x_turned_A"], at("x_turned_A", i))
                        ln_out("B", b_, acc["B"])
                    if s < len(us):
                        k, b, e = us[s]
                        eng.wait_ge(sem[f"y_rstd_{k}"], at(f"y_rstd_{k}", b, e + 1))
                        if s:
                            kk, bb, ee = us[s - 1]
                            eng.wait_ge(sem[f"y_turned_{kk}"], at(f"y_turned_{kk}", bb, 2 * ee + 2))
                        for j in range(2):
                            y = yhalf(s, j).rearrange("p (t n) -> p t n", t=2)
                            eng.tensor_tensor(yn[:, 2 * j:2 * j + 2, :], y,
                                                  rs1[k][:, 2 * j:2 * j + 2].unsqueeze(2).broadcast_to([P, 2, D]),
                                                  ALU.mult).then_inc(sem[f"y_normed_{k}"], 1)
                    if b_.live() and i.live() and s == 0:
                        add_attention(i, b_)
                    if m.live() and early and s == len(us):
                        reduce(m, 0)
                    if 1 <= s <= len(us):
                        k, b, e = us[s - 1]
                        if s >= 2:
                            kk, bb, ee = us[s - 2]
                            eng.wait_ge(sem[f"z_ready_{kk}"], at(f"z_ready_{kk}", bb, 2 * ee + 2))
                        for c in range(C):
                            eng.wait_ge(sem[f"h_ready_{k}"], at(f"h_ready_{k}", b, 2 * e + c + 1))
                            eng.wait_ge(sem[f"h_high_{k}"], at(f"h_high_{k}", b, 2 * e + c + 1))
                            eng.tensor_tensor(hl[:, c, :], hf[:, c, :], hh[:, c, :].bitcast(fp32),
                                              ALU.subtract).then_inc(sem[f"h_low_{k}"], 1)
                    for k, b in (("A", i), ("B", b_)):
                        if b.live() and s == step_gate(i, k):
                            gate_scores(i, k, b)
                    if i.live() and b_.live() and s == step_q(i):
                        low(i, "Q", i)
                    if m.live() and early and s == len(us) + 1:
                        reduce(m, 2)
                    if i.live() and b_.live() and s == step_q(i) - 3:
                        eng.wait_ge(sem["z_summed_A"], at("z_summed_A", i))
                        ln("Q", i, acc["A"])
                    if s >= 2:
                        k, b, e = us[s - 2]
                        eng.wait_ge(sem[f"z_factor_{k}"], at(f"z_factor_{k}", b, e + 1))
                        if s >= 3:
                            kk, bb, ee = us[s - 3]
                            eng.wait_ge(sem[f"z_summed_{kk}"], at(f"z_summed_{kk}", bb, ee + 1))
                        for t in range(T):
                            ins = eng.scalar_tensor_tensor(
                                out=u[:, t, :], in0=place(i, "z", s - 2, t // 2)[0][:, (t % 2) * D:(t % 2 + 1) * D],
                                scalar=wst[k][:, t:t + 1], in1=g2b[:, e, :], op0=ALU.mult, op1=ALU.mult)
                            if t % 2:
                                ins.then_inc(sem[f"z_scaled_{k}"], 1)
                        if k == "A":
                            if e == 0:
                                eng.wait_ge(sem["sum_begun_A"], at("sum_begun_A", b))
                            else:
                                eng.wait_ge(sem["z_summed_A"], at("z_summed_A", b, e))
                            shift(k, b, e)
                    if i.live() and b_.live() and s == step_q(i) - 2:
                        eng.wait_ge(sem["x_turned_B"], at("x_turned_B", b_))
                        ln_out("Q", i, acc["A"])
                    if m.live() and early and s == len(us):
                        reduce(m, 1)
                    for k, b in (("A", i), ("B", b_)):
                        if b.live() and s == step_gate(i, k) + 1:
                            gate_weights(k, b)
                    if b_.live() and i.live() and s == 2:
                        begin("B", b_)
                if m.live() and not early:
                    for h in range(LEAD):
                        reduce(m, h)
                if i.live() and not b_.live():
                    eng.wait_ge(sem["z_summed_A"], at("z_summed_A", i))
                    ln("Q", i, acc["A"])
                    ln_out("Q", i, acc["A"])
                    low(i, "Q", i)
                for h in range(H):
                    if m.live():
                        if h + LEAD < H:
                            reduce(m, h + LEAD)
                    if e_.live() and h % QUAD == QUAD - 1 and h >= QUAD:
                        normalise(e_, h // QUAD - 1)
                    if nxt.live() and h == 4:
                        eng.wait_ge(sem["x_loaded"], at("x_loaded", i))
                        ln("A", nxt, acc["A"])
                    if nxt.live() and h == 6:
                        eng.wait_ge(sem["x_turned_Q"], at("x_turned_Q", i))
                        ln_out("A", nxt, acc["A"])
                    if nxt.live() and h == 8:
                        begin("A", nxt)
                    if b_.live() and h in SHIFT_AT:
                        e = SHIFT_AT.index(h)
                        eng.wait_ge(sem["z_summed_B"], at("z_summed_B", b_))
                        if e:
                            eng.wait_ge(sem["z_shifted_B"], at("z_shifted_B", b_, e))
                        shift("B", b_, e)
                if m.live():
                    eng.wait_ge(sem["block_maxima"], at("block_maxima", m))
                    for t in range(T):
                        o = MCOL[t] // P
                        ins = eng.tensor_reduce(nm[:, t, :], bm[:, :, o:o + t + 1], AX.X, ALU.max, negate=True)
                    ins.then_inc(sem["maxima_ready"], 1)
                    eng.wait_ge(sem["maxima_ready"], at("maxima_ready", m))
                    eng.wait_ge(sem["maxima_turned"], at("maxima_turned", m - 1))
                    src = nm
                    for p in range(3):
                        eng.tensor_copy(nmp[:, :, p, :], src[:, :, :]).then_inc(sem["maxima_part"], 1)
                        if p < 2:
                            eng.wait_ge(sem["maxima_part"], at("maxima_part", m, p + 1))
                            eng.tensor_tensor(nmr[:, :, :], src[:, :, :], nmp[:, :, p, :], ALU.subtract).then_inc(sem["maxima_rest"], 1)
                            eng.wait_ge(sem["maxima_rest"], at("maxima_rest", m, p + 1))
                        src = nmr

                def rest(n_):
                    eng.wait_ge(sem["qk_part1"], at("qk_part1", i, n_ + 1))
                    if n_ >= 2:
                        eng.wait_ge(sem["qk_part3"], at("qk_part3", i, n_ - 1))
                    eng.tensor_tensor(qkr[:, n_ % 2, :], qkb[n_], qkp[n_ // C][:, 0, n_ % C, :],
                                      ALU.subtract).then_inc(sem["qk_rest"], 1)

                if i.live():
                    for j in range(2):
                        eng.wait_ge(sem["v_ready"], at("v_ready", i, j + 1))
                        eng.tensor_copy(va[i.s][:, 2 * j:2 * j + 2, :, 0:HD],
                                        bank[:, 3 + j, :].rearrange("p (t h d) -> p t h d", t=2, h=H)
                                        ).then_inc(sem["v_copied"], 1)
                        if j == 0:
                            rest(0)
                            rest(1)
                if e_.live():
                    normalise(e_, QUAD - 1)
                if nxt.live():
                    low(i, "A", nxt)
                if i.live():
                    rest(2)
                    rest(3)
                if e_.live():
                    low(i, "O", e_)

            def reduce(m, h):
                for p in range(2):
                    eng.wait_ge(sem["queries_scored"], at("queries_scored", m, 2 * h + p + 1))
                    eng.tensor_reduce(bm[:, h, PCOL[p] // P:PCOL[p + 1] // P],
                                      mps[:, PCOL[p]:PCOL[p + 1]].rearrange("p (b n) -> p b n", n=P),
                                      AX.X, ALU.max).then_inc(sem["block_maxima"], 1)

            def shift(k, b, e):
                for t in range(T):
                    ins = eng.scalar_tensor_tensor(
                        out=acc[k][:, t, :], in0=be2b[:, e, :], scalar=wgt[k][:, t, e:e + 1], in1=acc[k][:, t, :],
                        op0=ALU.mult, op1=ALU.add)
                ins.then_inc(sem[f"z_shifted_{k}"], 1)

            def normalise(b, g):
                if g == 0:
                    eng.wait_ge(sem["x_turned_O"], at("x_turned_O", b - 1))
                eng.wait_ge(sem["pv_turned"], at("pv_turned", b, g + 1))
                v = rps.rearrange("p (t q d) -> p t q d", t=T, q=QUAD)
                eng.reciprocal(rden[:, :, :], v[:, :, :, HD]).then_inc(sem["sums_inverted"], 1)
                eng.wait_ge(sem["sums_inverted"], at("sums_inverted", b, g + 1))
                eng.tensor_tensor(on[:, :, g * QUAD * HD:(g + 1) * QUAD * HD].rearrange("p t (q d) -> p t q d", q=QUAD),
                                      v[:, :, :, 0:HD], rden[:, :, :].unsqueeze(3).broadcast_to([P, T, QUAD, HD]),
                                      ALU.mult).then_inc(sem["pv_normed"], 1)

            step(eng.memset(on[:, 0:2, :], 0.0))
            eng.wait_ge(sem["first_x_loaded"], 16)
            ln("A", Seq(0), acc["A"])
            first_setup()
            eng.wait_ge(sem["pool_setup"], NPOOL_FIRST)
            ln_out("A", Seq(0), acc["A"])
            begin("A", Seq(0))
            second_setup()
            low(Seq(0), "A", Seq(0))
            rest_of_setup()
            drive(eng, iteration)


        @block.tensor
        def _(eng):
            eng.wait_ge(sem["pool_setup"], NPOOL_FIRST)
            PROD = ((0, 0), (0, 1), (1, 0))

            def xpose(i, k, b):
                eng.wait_ge(sem[f"ln_ready_{k}"], at(f"ln_ready_{k}", b))
                for c in range(C):
                    for t in range(T):
                        mm = eng.transpose(xps(i, k, c)[:, t * P:(t + 1) * P], xhat[:, t, c * P:(c + 1) * P], identf[:, :])
                    mm.then_inc(sem[f"x_turned_{k}"], 1)

            def tokens(out_, lhs, rhs, m=None, e=None):
                n = 0
                for c in range(C):
                    for a, w in PROD:
                        n += 1
                        mm = eng.matmul(out_, lhs(a, c), rhs(w, c), start=(n == 1),
                                        stop=(n == 3 * C and m is None))
                if m is not None:
                    mm = eng.matmul(out_, rows_of[:, e, :], bias[:, m, :], start=False, stop=True)
                return mm

            def gate_scores(i, k, b):
                out_, freed = place(i, "gate", k)
                if freed:
                    eng.wait_ge(sem[freed[0]], at(*freed))
                n = 0
                for c in range(C):
                    for a, w in PROD:
                        n += 1
                        mm = eng.matmul(out_[0:NEXP, :], gw[w][:, c, :], xt[k][a][:, c, :], start=(n == 1),
                                        stop=(n == 3 * C))
                mm.then_inc(sem[f"gate_ready_{k}"], 1)

            def gate_turn(i, k, b):
                out_ = place(i, "gate", k)[0]
                eng.wait_ge(sem[f"gate_biased_{k}"], at(f"gate_biased_{k}", b))
                settled(eng)
                for t in range(T):
                    mm = eng.transpose(out_[:, t * NEXP:(t + 1) * NEXP], gt[:, t * P:(t + 1) * P],
                                       identf[0:NEXP, 0:NEXP])
                mm.then_inc(sem[f"gate_turned_{k}"], 1)

            def project(i, b):
                for t in range(T):
                    out_, freed = place(i, "wo", t // 2)
                    if freed and t % 2 == 0:
                        eng.wait_ge(sem[freed[0]], at(*freed))
                    mm = tokens(out_[:, (t % 2) * D:(t % 2 + 1) * D],
                                lambda a, c: xt["O"][a][:, c, t * P:(t + 1) * P], lambda w, c: wo[w][:, c, :])
                    if t % 2:
                        mm.then_inc(sem["wo_ready"], 1)

            def turn_b(i, b):
                for c in range(C):
                    freed = place(i, "x", c)[1]
                    if freed:
                        eng.wait_ge(sem[freed[0]], at(*freed))
                xpose(i, "B", b)

            def zstep(i, us, s):
                k, b, e = us[s]
                eng.wait_ge(sem[f"h_low_{k}"], at(f"h_low_{k}", b, 2 * e + 2))
                hp = (hh, hl)
                for t in range(T):
                    out_, freed = place(i, "z", s, t // 2)
                    if freed and t % 2 == 0:
                        eng.wait_ge(sem[freed[0]], at(*freed))
                    mm = tokens(out_[:, (t % 2) * D:(t % 2 + 1) * D],
                                lambda a, c: hp[a][:, c, t * P:(t + 1) * P],
                                lambda w, c: w2[w][:, e, c, :], 1, e)
                    if t % 2:
                        mm.then_inc(sem[f"z_ready_{k}"], 1)

            def maxima(m, h):
                for p in range(2):
                    if h:
                        eng.wait_ge(sem["block_maxima"], at("block_maxima", m, 2 * h - 1 + p))
                    for t in MPART[p]:
                        o = MCOL[t]
                        w_ = (t + 1) * P
                        eng.matmul(mps[:, o:o + w_], qs[m.s][0:KR, h, t * P:(t + 1) * P], ks[m.s][0:KR, h, 0:w_],
                                   start=True, stop=False)
                        mm = eng.matmul(mps[:, o + w_ - P:o + w_], identb[:, :], mask_q[:, :], start=False,
                                        stop=True)
                    mm.then_inc(sem["queries_scored"], 1)

            def iteration(i):
                us = units(i)
                b_ = i - 3
                m, e_ = i - 1, i - 2

                def chunk(n_):
                    n = 0
                    for c in range(C):
                        for a, w in PROD:
                            n += 1
                            mm = eng.matmul(qkb[n_], wqkv[w][:, c, n_ * P:(n_ + 1) * P],
                                            xt["Q"][a][:, c, :], start=(n == 1), stop=(n == 3 * C))
                    mm.then_inc(sem["qk_ready"], 1)

                early = b_.live() or not i.live()
                if i.live():
                    eng.wait_ge(sem["x_low_A"], at("x_low_A", i))
                if i.n == 0:
                    eng.wait_ge(sem["dve_setup"], NDVE_FIRST)
                for s in range(len(us) + 2):
                    if i.n == 0 and s == 2:
                        eng.wait_ge(sem["dve_setup"], NDVE)
                        eng.wait_ge(sem["pool_setup"], NPOOL)
                    if b_.live() and not i.live() and s == 0:
                        if (i - 1).live():
                            eng.wait_ge(sem["qk_rest"], at("qk_rest", i - 1))
                        project(i, b_)
                        turn_b(i, b_)
                        eng.wait_ge(sem["x_low_B"], at("x_low_B", b_))
                        gate_scores(i, "B", b_)
                    if i.live() and b_.live() and s == step_q(i):
                        k, b, e = us[-1]
                        eng.wait_ge(sem[f"h_high_{k}"], at(f"h_high_{k}", b))
                        xpose(i, "Q", i)
                    if s < len(us):
                        k, b, e = us[s]
                        if e == 0 and k == "B":
                            eng.wait_ge(sem["x_low_B"], at("x_low_B", b))
                        for t in range(T):
                            if t % 2 == 0 and 2 * s + t // 2 >= 3:
                                kk, bb, ee = us[(2 * s + t // 2 - 3) // 2]
                                v = 2 * ee + (2 * s + t // 2 - 3) % 2 + 1
                                eng.wait_ge(sem[f"y_normed_{kk}"], at(f"y_normed_{kk}", bb, v))
                            mm = tokens(yhalf(s, t // 2)[:, (t % 2) * D:(t % 2 + 1) * D],
                                        lambda a, c: xt[k][a][:, c, t * P:(t + 1) * P],
                                        lambda w, c: w1[w][:, e, c, :], 0, e)
                            if t % 2:
                                mm.then_inc(sem[f"y_ready_{k}"], 1)
                    if i.live() and s == 0:
                        if (i - 1).live():
                            eng.wait_ge(sem["qk_rest"], at("qk_rest", i - 1))
                        gate_scores(i, "A", i)
                        if b_.live():
                            eng.wait_ge(sem["x_low_O"], at("x_low_O", b_))
                            project(i, b_)
                        gate_turn(i, "A", i)
                    if b_.live() and i.live() and s == step_xb(i):
                        turn_b(i, b_)
                    if b_.live() and i.live() and s == step_gate(i, "B"):
                        eng.wait_ge(sem["x_low_B"], at("x_low_B", b_))
                        gate_scores(i, "B", b_)
                    if 1 <= s <= len(us):
                        k, b, e = us[s - 1]
                        eng.wait_ge(sem[f"y_normed_{k}"], at(f"y_normed_{k}", b, 2 * e + 2))
                        if s >= 2:
                            kk, bb, ee = us[s - 2]
                            eng.wait_ge(sem[f"h_high_{kk}"], at(f"h_high_{kk}", bb, 2 * ee + 2))
                        for c in range(C):
                            for t in range(T):
                                mm = eng.transpose(tps[:, c, t * P:(t + 1) * P], yn[:, t, c * P:(c + 1) * P],
                                                   identf[:, :])
                            mm.then_inc(sem[f"y_turned_{k}"], 1)
                    if m.live() and early and s == len(us):
                        eng.wait_ge(sem["stacks_placed"], at("stacks_placed", m))
                        maxima(m, 0)
                    if s >= 2:
                        zstep(i, us, s - 2)
                    if m.live() and early and s >= len(us):
                        maxima(m, s - len(us) + 1)
                    if b_.live() and s == step_gate(i, "B"):
                        gate_turn(i, "B", b_)
                if m.live() and not early:
                    eng.wait_ge(sem["stacks_placed"], at("stacks_placed", m))
                    for h in range(LEAD):
                        maxima(m, h)
                if i.live() and not b_.live():
                    k, b, e = us[-1]
                    eng.wait_ge(sem[f"h_high_{k}"], at(f"h_high_{k}", b))
                    xpose(i, "Q", i)
                for h in range(H):
                    if m.live() and h + LEAD < H:
                        maxima(m, h + LEAD)
                    if h == 0:
                        for k, b, e in us[-2:]:
                            eng.wait_ge(sem[f"y_normed_{k}"], at(f"y_normed_{k}", b))
                            eng.wait_ge(sem[f"z_scaled_{k}"], at(f"z_scaled_{k}", b))
                        if i.live():
                            eng.wait_ge(sem["x_low_Q"], at("x_low_Q", i))
                    for p in range(2):
                        if e_.live():
                            if h:
                                eng.wait_ge(sem["exp_ready"], at("exp_ready", e_, 2 * h - 1 + p))
                            elif p == 0:
                                eng.wait_ge(sem["maxima_placed"], at("maxima_placed", e_))
                                eng.wait_ge(sem["v_copied"], at("v_copied", e_))
                            for j in EPART[p]:
                                o = ECOL[j]
                                w_ = S - j * P
                                eng.matmul(eps_[:, o:o + w_], ks[e_.s][0:KR + 3, h, j * P:(j + 1) * P],
                                           qs[e_.s][0:KR + 3, h, j * P:S], start=True, stop=False)
                                mm = eng.matmul(eps_[:, o:o + P], identb[:, :], mask_k[:, :], start=False, stop=True)
                            mm.then_inc(sem["keys_scored"], 1)
                    if i.live() and h + LEAD >= H:
                        if m.live():
                            eng.wait_ge(sem["block_maxima"], at("block_maxima", m))
                        chunk(h + LEAD - H)
                    if e_.live():
                        if h % QUAD == 0 and h >= QUAD:
                            pv(e_, h // QUAD - 1)
                        if h % QUAD == 2 and h >= QUAD:
                            o_back(e_, h // QUAD - 1)
                nxt = Seq(i.n + 1, i.reg)

                if e_.live():
                    pv(e_, QUAD - 1)
                if m.live():
                    eng.wait_ge(sem["maxima_part"], at("maxima_part", m))
                    settled(eng)
                    m16 = mt.bitcast(bf16)
                    for t in range(T):
                        mm = eng.transpose(m16[0:3 * H, t * P:(t + 1) * P],
                                           nmp[:, t, :, :].rearrange("p a h -> p (a h)"), identb[:, :])
                    mm.then_inc(sem["maxima_turned"], 1)
                if i.live():
                    for t in range(T):
                        mm = tokens(bank[:, 3 + t // 2, (t % 2) * D:(t % 2 + 1) * D],
                                    lambda a, c: xt["Q"][a][:, c, t * P:(t + 1) * P],
                                    lambda w, c: wqkv[w][:, c, 2 * D:3 * D])
                        if t % 2:
                            mm.then_inc(sem["v_ready"], 1)
                if e_.live():
                    o_back(e_, QUAD - 1)
                if i.live():
                    if m.live():
                        eng.wait_ge(sem["maxima_copied"], at("maxima_copied", m))
                    for n_ in range(LEAD, 2 * C):
                        chunk(n_)
                if nxt.live():
                    if i.live():
                        eng.wait_ge(sem["v_copied"], at("v_copied", i))
                    xpose(i, "A", nxt)
                if e_.live():
                    eng.wait_ge(sem["pv_normed"], at("pv_normed", e_))
                    for c in range(C):
                        for t in range(T):
                            mm = eng.transpose(xps(i, "O", c)[:, t * P:(t + 1) * P], on[:, t, c * P:(c + 1) * P],
                                               identf[:, :])
                        mm.then_inc(sem["x_turned_O"], 1)
                if i.live():
                    eng.wait_ge(sem["qk_rest"], at("qk_rest", i, 3))
                if e_.live() and not nxt.live():
                    eng.wait_ge(sem["x_low_O"], at("x_low_O", e_))
                if m.live():
                    eng.wait_ge(sem["maxima_copied"], at("maxima_copied", m))

            def pv(b, g):
                eng.wait_ge(sem["exp_ready"], at("exp_ready", b, 2 * (g + 1) * QUAD))
                if g:
                    eng.wait_ge(sem["pv_copied"], at("pv_copied", b, g))
                for j in range(T):
                    for q in range(QUAD):
                        h = g * QUAD + q
                        mm = eng.matmul(ops[q * 32:q * 32 + HD + 1, j * P:S], va[b.s][:, j, h, :],
                                        pt[:, h % NPT, ECOL[j]:ECOL[j] + S - j * P],
                                        start=(j == 0), stop=(j == T - 1))
                mm.then_inc(sem["pv_ready"], 1)

            def o_back(b, g):
                eng.wait_ge(sem["pv_copied"], at("pv_copied", b, g + 1))
                if g:
                    eng.wait_ge(sem["pv_normed"], at("pv_normed", b, g))
                for t in range(T):
                    mm = eng.transpose(rps[:, t * P:(t + 1) * P], ot[:, t * P:(t + 1) * P], identf[:, :])
                mm.then_inc(sem["pv_turned"], 1)

            xpose(Seq(0), "A", Seq(0))
            drive(eng, iteration)


_INS = ['L0_attn_x', 'L0_attn_Wq', 'L0_attn_Wkv', 'L0_attn_Wo', 'L0_ffn_gate_W', 'L0_ffn_gate_b', 'L0_ffn_W1',
        'L0_ffn_b1', 'L0_ffn_g1', 'L0_ffn_be1', 'L0_ffn_W2', 'L0_ffn_b2', 'L0_ffn_g2', 'L0_ffn_be2']


def kernel(**inputs):
    import numpy as _np
    import concourse.bacc as _bacc
    from concourse import mybir as _mybir
    from concourse.bass_utils import run_bass_kernel_spmd as _run

    nc = _bacc.Bacc("TRN2", target_bir_lowering=False, num_devices=1)
    arrays, args = {}, []
    for name in _INS:
        a = _np.ascontiguousarray(inputs[name])
        arrays[f"in_{name}_dram"] = a
        args.append(nc.dram_tensor(f"in_{name}_dram", a.shape, _mybir.dt.from_np(a.dtype), kind="ExternalInput").ap())
    shape = inputs['L0_attn_x'].shape
    args.append(nc.dram_tensor("out_0_dram", shape, _mybir.dt.float32, kind="ExternalOutput").ap())
    macaron_kernel(nc, *args)
    r = _run(nc, [arrays], core_ids=[0])
    return r.results[0]["out_0_dram"]
```
